# Optimizing a Trainium2 kernel written in Bass

```python
import numpy as np
import jax
import jax.numpy as jnp

def _softmax(x, axis=-1):
    return jax.nn.softmax(x, axis=axis)
def _gelu(x):
    return jax.nn.gelu(x, approximate=True)
def _silu(x):
    return jax.nn.silu(x)
def _sigmoid(x):
    return jax.nn.sigmoid(x)
def _layernorm(x, axis=-1, eps=1e-5):
    m = jnp.mean(x, axis=axis, keepdims=True)
    v = jnp.var(x, axis=axis, keepdims=True)
    return (x - m) / jnp.sqrt(v + eps)
def _scatter_add(tgt, idx, src, axis=0):
    return tgt.at[idx].add(src)
def _segment_sum(src, seg, n):
    return jax.ops.segment_sum(src, seg, n)

kernel_name = 'mk_conv_attn_hybrid_d2_conv_nhwc256_9a074c'

def setup_inputs(seed: int = 0):
    np.random.seed(seed)
    _w = jnp.asarray
    def _rec_inputs():
        import jax
        import jax.numpy as jnp
        _gk = jax.random.key(seed)
        x = -0.0009896 + 1 * jax.random.normal(jax.random.fold_in(_gk, 1), (2, 56, 56, 256), jnp.float32)
        return x
    x = _rec_inputs()
    def _L0_conv_setup():
        import jax, jax.numpy as jnp
        import numpy as np
        N_HEADS = 8
        WINDOW = 7

        def _conv1x1(x, W, b):
            return jnp.einsum('bhwc,cd->bhwd', x, W) + b

        def _to_heads(t, nh):
            B, H, W, C = t.shape
            return jnp.transpose(t, (0, 3, 1, 2)).reshape(B, nh, C // nh, H * W)
        key = jax.random.key(seed)
        ks = jax.random.split(key, 8)
        B, H, W, C = (2, 56, 56, 256)
        x = jax.random.normal(ks[0], (B, H, W, C), dtype=jnp.float32)
        s = 1.0 / np.sqrt(C)
        Wq = jax.random.normal(ks[1], (C, C), dtype=jnp.float32) * s
        bq = jnp.zeros((C,), dtype=jnp.float32)
        Wk = jax.random.normal(ks[2], (C, C), dtype=jnp.float32) * s
        bk = jnp.zeros((C,), dtype=jnp.float32)
        Wv = jax.random.normal(ks[3], (C, C), dtype=jnp.float32) * s
        bv = jnp.zeros((C,), dtype=jnp.float32)
        gamma = jax.random.normal(ks[4], (1,), dtype=jnp.float32) * 0.1
        return {'x': x, 'Wq': Wq, 'bq': bq, 'Wk': Wk, 'bk': bk, 'Wv': Wv, 'bv': bv, 'gamma': gamma}
    _L0_conv_all = _L0_conv_setup()
    _L0_conv_in = {k: v for k, v in _L0_conv_all.items() if k in ('Wq', 'bq', 'Wk', 'bk', 'Wv', 'bv', 'gamma', )}
    del _L0_conv_all

    def _L1_attn_setup():
        import jax, jax.numpy as jnp
        import numpy as np
        S, B, F = (2048, 16, 256)
        key = jax.random.key(seed)
        ks = jax.random.split(key, 7)
        scale = 1.0 / np.sqrt(F)
        return {'x': jax.random.normal(ks[0], (S, B, F), dtype=jnp.float32), 'Wq': jax.random.normal(ks[1], (F, F), dtype=jnp.float32) * scale, 'bq': jax.random.normal(ks[2], (F,), dtype=jnp.float32) * 0.01, 'Wk': jax.random.normal(ks[3], (F, F), dtype=jnp.float32) * scale, 'bk': jax.random.normal(ks[4], (F,), dtype=jnp.float32) * 0.01, 'Wv': jax.random.normal(ks[5], (F, F), dtype=jnp.float32) * scale, 'bv': jax.random.normal(ks[6], (F,), dtype=jnp.float32) * 0.01}
    _L1_attn_all = _L1_attn_setup()
    _L1_attn_in = {k: v for k, v in _L1_attn_all.items() if k in ('Wq', 'bq', 'Wk', 'bk', 'Wv', 'bv', )}
    del _L1_attn_all

    def _L1_ffn_setup():
        import jax, jax.numpy as jnp
        import numpy as np
        B, N, D = (16, 4096, 256)
        NUM_EXPERTS, TOP_K, HEADS = (4, 2, 4)
        N_EDGES = 1048576
        LN_EPS = 1e-05

        def _layernorm(x, g, b):
            mu = x.mean(-1, keepdims=True)
            var = ((x - mu) ** 2).mean(-1, keepdims=True)
            return (x - mu) * jax.lax.rsqrt(var + LN_EPS) * g + b

        def _forward(x, edge_index, W_gat, att_src, att_dst, b_gat, ln_gamma, ln_beta, W1, b1, W2, b2):
            Bc, Nc, Dc = x.shape
            M = Bc * Nc
            x_flat = x.reshape(M, Dc)
            h = (x_flat @ W_gat).reshape(M, HEADS, NUM_EXPERTS)
            loops = jnp.arange(M, dtype=edge_index.dtype)
            src = jnp.concatenate([edge_index[0], loops])
            dst = jnp.concatenate([edge_index[1], loops])
            a_src = (h * att_src).sum(-1)
            a_dst = (h * att_dst).sum(-1)
            e = jax.nn.leaky_relu(a_src[src] + a_dst[dst], negative_slope=0.2)
            e_max = jax.ops.segment_max(e, dst, num_segments=M)
            ee = jnp.exp(e - e_max[dst])
            denom = jax.ops.segment_sum(ee, dst, num_segments=M)
            alpha = ee / (denom[dst] + 1e-16)
            msg = h[src] * alpha[:, :, None]
            agg = jax.ops.segment_sum(msg, dst, num_segments=M).reshape(M, HEADS * NUM_EXPERTS) + b_gat
            scores = _layernorm(agg, ln_gamma, ln_beta).reshape(M, HEADS, NUM_EXPERTS).mean(1)
            scores = scores.reshape(Bc, Nc, NUM_EXPERTS)
            topk_s, topk_i = jax.lax.top_k(scores, TOP_K)
            w = jax.nn.softmax(topk_s, axis=-1)
            out = jnp.zeros_like(x)
            for ei in range(NUM_EXPERTS):
                g = jnp.where(topk_i == ei, w, 0.0).sum(-1)
                hh = jax.nn.gelu(x @ W1[ei] + b1[ei], approximate=False)
                out = out + g[..., None] * (hh @ W2[ei] + b2[ei])
            return out
        key = jax.random.key(seed)
        ks = jax.random.split(key, 8)
        s = 0.05
        return {'x': jax.random.normal(ks[0], (B, N, D), jnp.float32), 'W_gat': jax.random.normal(ks[1], (D, HEADS * NUM_EXPERTS), jnp.float32) * s, 'att_src': jax.random.normal(ks[2], (HEADS, NUM_EXPERTS), jnp.float32) * s, 'att_dst': jax.random.normal(ks[3], (HEADS, NUM_EXPERTS), jnp.float32) * s, 'b_gat': jnp.zeros((HEADS * NUM_EXPERTS,), jnp.float32), 'ln_gamma': jnp.ones((HEADS * NUM_EXPERTS,), jnp.float32), 'ln_beta': jnp.zeros((HEADS * NUM_EXPERTS,), jnp.float32), 'W1': jax.random.normal(ks[4], (NUM_EXPERTS, D, 2 * D), jnp.float32) * s, 'b1': jnp.zeros((NUM_EXPERTS, 2 * D), jnp.float32), 'W2': jax.random.normal(ks[5], (NUM_EXPERTS, 2 * D, D), jnp.float32) * s, 'b2': jnp.zeros((NUM_EXPERTS, D), jnp.float32), 'edge_index': jax.random.randint(ks[6], (2, N_EDGES), 0, B * N, jnp.int32)}
    _L1_ffn_all = _L1_ffn_setup()
    _L1_ffn_in = {k: v for k, v in _L1_ffn_all.items() if k in ('W_gat', 'att_src', 'att_dst', 'b_gat', 'ln_gamma', 'ln_beta', 'W1', 'b1', 'W2', 'b2', 'edge_index', )}
    del _L1_ffn_all

    return {
        "x": x,
        "L0_conv_Wq": _L0_conv_in["Wq"],
        "L0_conv_bq": _L0_conv_in["bq"],
        "L0_conv_Wk": _L0_conv_in["Wk"],
        "L0_conv_bk": _L0_conv_in["bk"],
        "L0_conv_Wv": _L0_conv_in["Wv"],
        "L0_conv_bv": _L0_conv_in["bv"],
        "L0_conv_gamma": _L0_conv_in["gamma"],
        "L1_attn_Wq": _L1_attn_in["Wq"],
        "L1_attn_bq": _L1_attn_in["bq"],
        "L1_attn_Wk": _L1_attn_in["Wk"],
        "L1_attn_bk": _L1_attn_in["bk"],
        "L1_attn_Wv": _L1_attn_in["Wv"],
        "L1_attn_bv": _L1_attn_in["bv"],
        "L1_ffn_W_gat": _L1_ffn_in["W_gat"],
        "L1_ffn_att_src": _L1_ffn_in["att_src"],
        "L1_ffn_att_dst": _L1_ffn_in["att_dst"],
        "L1_ffn_b_gat": _L1_ffn_in["b_gat"],
        "L1_ffn_ln_gamma": _L1_ffn_in["ln_gamma"],
        "L1_ffn_ln_beta": _L1_ffn_in["ln_beta"],
        "L1_ffn_W1": _L1_ffn_in["W1"],
        "L1_ffn_b1": _L1_ffn_in["b1"],
        "L1_ffn_W2": _L1_ffn_in["W2"],
        "L1_ffn_b2": _L1_ffn_in["b2"],
        "L1_ffn_edge_index": _L1_ffn_in["edge_index"],
    }

def reference(x, L0_conv_Wq, L0_conv_bq, L0_conv_Wk, L0_conv_bk, L0_conv_Wv, L0_conv_bv, L0_conv_gamma, L1_attn_Wq, L1_attn_bq, L1_attn_Wk, L1_attn_bk, L1_attn_Wv, L1_attn_bv, L1_ffn_W_gat, L1_ffn_att_src, L1_ffn_att_dst, L1_ffn_b_gat, L1_ffn_ln_gamma, L1_ffn_ln_beta, L1_ffn_W1, L1_ffn_b1, L1_ffn_W2, L1_ffn_b2, L1_ffn_edge_index):
    import jax
    import jax.numpy as jnp
    def _L0_conv_ref(x, Wq, bq, Wk, bk, Wv, bv, gamma):
        import jax, jax.numpy as jnp
        import numpy as np
        N_HEADS = 8
        WINDOW = 7

        def _conv1x1(x, W, b):
            return jnp.einsum('bhwc,cd->bhwd', x, W) + b

        def _to_heads(t, nh):
            B, H, W, C = t.shape
            return jnp.transpose(t, (0, 3, 1, 2)).reshape(B, nh, C // nh, H * W)
        B, H, W, C = x.shape
        p = WINDOW // 2
        xp = jnp.pad(x, ((0, 0), (p, p), (p, p), (0, 0)), mode='reflect')
        q = _to_heads(_conv1x1(x, Wq, bq), N_HEADS)
        k = _to_heads(_conv1x1(xp, Wk, bk), N_HEADS)
        v = _to_heads(_conv1x1(xp, Wv, bv), N_HEADS)
        energy = jnp.einsum('bhdq,bhdk->bhqk', q, k)
        attn = jax.nn.softmax(energy, axis=-1)
        out = jnp.einsum('bhdk,bhqk->bhdq', v, attn)
        out = out.reshape(B, C, H, W).transpose(0, 2, 3, 1)
        return gamma * out + x

    def _L1_attn_ref(x, Wq, bq, Wk, bk, Wv, bv):
        import jax, jax.numpy as jnp
        import numpy as np
        S, B, F = (2048, 16, 256)
        n_features = x.shape[-1]
        Q = jnp.einsum('sbf,gf->sbg', x, Wq) + bq
        K = jnp.einsum('sbf,gf->sbg', x, Wk) + bk
        V = jnp.einsum('sbf,gf->sbg', x, Wv) + bv
        scores = jnp.einsum('sbf,tbf->bst', Q, K) / jnp.sqrt(jnp.asarray(n_features, dtype=x.dtype))
        attn = jax.nn.softmax(scores, axis=-1)
        out = jnp.einsum('bst,tbf->sbf', attn, V)
        return out

    def _L1_ffn_ref(x, W_gat, att_src, att_dst, b_gat, ln_gamma, ln_beta, W1, b1, W2, b2, edge_index):
        import jax, jax.numpy as jnp
        import numpy as np
        B, N, D = (16, 4096, 256)
        NUM_EXPERTS, TOP_K, HEADS = (4, 2, 4)
        N_EDGES = 1048576
        LN_EPS = 1e-05

        def _layernorm(x, g, b):
            mu = x.mean(-1, keepdims=True)
            var = ((x - mu) ** 2).mean(-1, keepdims=True)
            return (x - mu) * jax.lax.rsqrt(var + LN_EPS) * g + b

        def _forward(x, edge_index, W_gat, att_src, att_dst, b_gat, ln_gamma, ln_beta, W1, b1, W2, b2):
            Bc, Nc, Dc = x.shape
            M = Bc * Nc
            x_flat = x.reshape(M, Dc)
            h = (x_flat @ W_gat).reshape(M, HEADS, NUM_EXPERTS)
            loops = jnp.arange(M, dtype=edge_index.dtype)
            src = jnp.concatenate([edge_index[0], loops])
            dst = jnp.concatenate([edge_index[1], loops])
            a_src = (h * att_src).sum(-1)
            a_dst = (h * att_dst).sum(-1)
            e = jax.nn.leaky_relu(a_src[src] + a_dst[dst], negative_slope=0.2)
            e_max = jax.ops.segment_max(e, dst, num_segments=M)
            ee = jnp.exp(e - e_max[dst])
            denom = jax.ops.segment_sum(ee, dst, num_segments=M)
            alpha = ee / (denom[dst] + 1e-16)
            msg = h[src] * alpha[:, :, None]
            agg = jax.ops.segment_sum(msg, dst, num_segments=M).reshape(M, HEADS * NUM_EXPERTS) + b_gat
            scores = _layernorm(agg, ln_gamma, ln_beta).reshape(M, HEADS, NUM_EXPERTS).mean(1)
            scores = scores.reshape(Bc, Nc, NUM_EXPERTS)
            topk_s, topk_i = jax.lax.top_k(scores, TOP_K)
            w = jax.nn.softmax(topk_s, axis=-1)
            out = jnp.zeros_like(x)
            for ei in range(NUM_EXPERTS):
                g = jnp.where(topk_i == ei, w, 0.0).sum(-1)
                hh = jax.nn.gelu(x @ W1[ei] + b1[ei], approximate=False)
                out = out + g[..., None] * (hh @ W2[ei] + b2[ei])
            return out
        return _forward(x, edge_index, W_gat, att_src, att_dst, b_gat, ln_gamma, ln_beta, W1, b1, W2, b2)

    def _gn(v, G=32, eps=1e-5):
        B_, H_, W_, C_ = v.shape
        g = v.reshape(B_, H_, W_, G, C_ // G)
        m = jnp.mean(g, axis=(1, 2, 4), keepdims=True)
        s = jnp.var(g, axis=(1, 2, 4), keepdims=True)
        return ((g - m) / jnp.sqrt(s + eps)).reshape(v.shape)

    def _ln_c(v, eps=1e-6):
        m = jnp.mean(v, axis=-1, keepdims=True)
        s = jnp.var(v, axis=-1, keepdims=True)
        return (v - m) / jnp.sqrt(s + eps)

    def _ln_t(v, eps=1e-5):
        m = jnp.mean(v, axis=-1, keepdims=True)
        s = jnp.var(v, axis=-1, keepdims=True)
        return (v - m) / jnp.sqrt(s + eps)

    def _to_tokens(v):
        B_, H_, W_, C_ = v.shape
        return v.reshape(B_, H_ * W_, C_)
    def _from_tokens(t, like):
        return t.reshape(like.shape)

    x = _L0_conv_ref(x, L0_conv_Wq, L0_conv_bq, L0_conv_Wk, L0_conv_bk, L0_conv_Wv, L0_conv_bv, L0_conv_gamma)
    t = _to_tokens(x)
    t = t + _L1_attn_ref(_ln_t(t), L1_attn_Wq, L1_attn_bq, L1_attn_Wk, L1_attn_bk, L1_attn_Wv, L1_attn_bv)
    t = t + _L1_ffn_ref(_ln_t(t), L1_ffn_W_gat, L1_ffn_att_src, L1_ffn_att_dst, L1_ffn_b_gat, L1_ffn_ln_gamma, L1_ffn_ln_beta, L1_ffn_W1, L1_ffn_b1, L1_ffn_W2, L1_ffn_b2, L1_ffn_edge_index)
    x = _from_tokens(t, x)
    return x


_drawn_inputs = setup_inputs


def setup_inputs(seed=0):
    import zlib

    import numpy as np

    out = dict(_drawn_inputs(seed))
    spreads = {'L0_conv_bq': (0.0, 0.412),
     'L0_conv_bk': (0.0, 2.0),
     'L0_conv_bv': (0.0, 0.542),
     'L1_ffn_b_gat': (0.0, 0.1),
     'L1_ffn_ln_gamma': (1.0, 0.6),
     'L1_ffn_ln_beta': (0.0, 0.507),
     'L1_ffn_b1': (0.0, 0.1),
     'L1_ffn_b2': (0.0, 0.1)}
    factors = {'L1_attn_bq': 8.0,
     'L1_attn_bk': 64.0,
     'L1_attn_bv': 4.993,
     'L1_ffn_att_src': 27.228,
     'L1_ffn_att_dst': 33.864}
    for name, (base, spread) in spreads.items():
        noise = np.random.default_rng([zlib.crc32(name.encode()), seed]).standard_normal(out[name].shape)
        drawn = base * np.exp(spread * noise) if base else spread * noise
        out[name] = jnp.asarray(drawn.astype(out[name].dtype))
    for name, factor in factors.items():
        out[name] = (out[name] * factor).astype(out[name].dtype)
    return out
```

```python
import numpy as np

import concourse.bass as bass
from concourse import mybir
from contextlib import ExitStack

F32 = mybir.dt.float32
BF16 = mybir.dt.bfloat16
I32 = mybir.dt.int32
U32 = mybir.dt.uint32
ALU = mybir.AluOpType
ACT = mybir.ActivationFunctionType
AX = mybir.AxisListType

P = 128
B, SIDE, C = 2, 56, 256
NTOK = SIDE * SIDE
M = B * NTOK
HEADS, HD = 8, 32
CH = 448
NCH = NTOK // CH
QT = 112
TPC = CH // QT
TILES = M // QT
KT = (NTOK + P - 1) // P
KPAD = KT * P
VW = HD + 1
NIT = B * HEADS * NCH
EDGES = 1048576
ECOLS = EDGES // P
GC = 7
EPI = 11
SLOTS = EPI + 2
ITC = EPI * GC
ALLC = NIT * ITC
PG = 56
PC = PG * GC
NPIECE = ALLC // PC
FULLP = ECOLS // PC
K = 40
DHI = M // P
BIG = 1.0e7
GH, GE = 4, 4
GF = GH * GE
ROW = GF + 2 * GH
FF = 512
LN_EPS = 1e-5


class Tally:

    def __init__(self, sem, base=0):
        self.sem, self.base, self.k = sem, base, 0

    def inc(self, ins):
        self.k += 1
        ins.then_inc(self.sem, 1)
        return self.k

    def value(self):
        return self.base + self.k


def build(nc, a, out):
    ctx = ExitStack()
    with ctx:
        def dram(name, shape, dt):
            return nc.dram_tensor(name, shape, dt).ap()

        s = {
            "q": dram("q_parts", [3, B * C, NTOK], BF16),
            "k": dram("k_parts", [3, B * C, KPAD], BF16),
            "v": dram("v_rows", [B * HEADS, P, KT * VW], F32),
            "pay": dram("edge_payload", [P, ALLC * 4], BF16),
            "src": dram("sources_by_target", [M * K, 1], I32),
            "node": dram("node_rows", [M + 1, ROW], F32),
        }
        xtok = ctx.enter_context(nc.sbuf_tensor("xtok", [QT, TILES, C], F32))
        mid = ExitStack()
        with mid:
            pos = mid.enter_context(nc.sbuf_tensor("pos", [P, ALLC + 2 * GC], BF16))
            prepare(nc, a, s, xtok, pos)
            attend(nc, a, s, xtok, pos)
        xhT = ctx.enter_context(nc.sbuf_tensor("xhT", [P, 2, M], F32))
        nodes = ctx.enter_context(nc.sbuf_tensor("nodes", [QT, TILES, ROW], F32))
        mix(nc, a, s, xtok, xhT, nodes)
        route(nc, a, s, xtok, xhT, nodes, out)


def prepare(nc, a, s, xtok, pos):
    ctx = ExitStack()
    with ctx:
        def sb(name, shape, dt):
            return ctx.enter_context(nc.sbuf_tensor(name, shape, dt))

        def pb(name):
            return ctx.enter_context(nc.psum_tensor(name, [P, 512], F32))

        def sem(name):
            return ctx.enter_context(nc.semaphore(name))

        xT = sb("xT", [P, 2, KPAD], F32)
        w = sb("w0", [P, 3, 2, C], F32)
        qkb = sb("qkb", [P, 2, 2], F32)
        bvb = sb("bvb", [P, C], F32)
        wk = sb("wk", [P, KT], F32)
        identf = sb("identf0", [P, P], F32)
        before = sb("before0", [P, P], BF16)
        full = sb("full", [P, 2, CH], F32)
        rest = sb("rest", [P, 2, CH], F32)
        parts = sb("parts", [P, 2, 3, CH], BF16)
        vtmp = sb("vtmp", [P, 2, C], F32)
        vrow = sb("vrow", [P, HEADS, KT, VW], F32)
        none = sb("none", [QT, TILES * K], I32)
        raw = sb("raw", [P, 2, 2, PC], I32)
        e1 = sb("e1", [P, PC], F32)
        ev = sb("ev", [P, PC], F32)
        eh = sb("eh", [P, PC], I32)
        es = sb("es", [P, PC], F32)
        esi = sb("esi", [P, PC], I32)
        esh = sb("esh", [P, PC], I32)
        pre = sb("pre", [P, PG, GC], F32)
        sums = sb("sums", [P, PG], BF16)
        pay = sb("pay0", [P, 2, PC, 4], BF16)
        p_t = [pb("p_t0"), pb("p_t1")]
        p_p = [pb("p_p0"), pb("p_p1")]
        p_v = [pb("p_v0"), pb("p_v1")]
        p_b = pb("p_base")

        x_in = [sem(f"x_in{b}") for b in range(B)]
        w_in = sem("w_in")
        const = sem("const")
        zeroed = sem("zeroed")
        turned = sem("turned")
        xt_ok = sem("xt_ok")
        proj = sem("proj")
        full_ok = sem("full_ok")
        p1_ok = sem("p1_ok")
        p2_ok = sem("p2_ok")
        rest_ok = sem("rest_ok")
        p3_ok = sem("p3_ok")
        parts_out = [sem(f"parts_out{i}") for i in range(2)]
        v_ps = sem("v_ps")
        v_sum = sem("v_sum")
        v_ok = sem("v_ok")
        v_out = sem("v_out")
        none_ok = sem("none_ok")
        none_out = sem("none_out")
        raw_in = [sem(f"raw_in{i}") for i in range(2)]
        sums_ok = sem("sums_ok")
        base_ok = sem("base_ok")
        own = sem("own0")
        pay_ok = sem("pay_ok")
        pay_out = [sem(f"pay_out{i}") for i in range(2)]

        NG = 2 * NCH
        NP = 2 * 2 * NCH
        edge_v = a["edge"].rearrange("a (p c) -> p a c", p=P)
        x_v = a["x"].rearrange("b h w c -> b (h w) c").rearrange("b (t p) c -> b p t c", p=QT)
        tb = TILES // B
        LASTC = ECOLS - FULLP * PC

        block = ctx.enter_context(nc.Block())

        @block.sync
        def _(sp):
            for b in range(B):
                sp.dma_start(xtok[:, b * tb:(b + 1) * tb, :], x_v[b]).then_inc(x_in[b], 16)
            for i, name in enumerate(("Wq", "Wk", "Wv")):
                sp.dma_start(w[:, i], a[name].rearrange("(t p) n -> p t n", p=P)).then_inc(w_in, 16)
            for i, name in enumerate(("bq", "bk")):
                sp.dma_start(qkb[:, i, :], a[name].rearrange("(m p) -> p m", p=P),
                             allow_slow_non_contiguous=True).then_inc(w_in, 16)
            sp.dma_start(bvb[:], a["bv"].partition_broadcast(P)).then_inc(w_in, 16)
            sp.dma_start(wk[:], a["mult"]).then_inc(w_in, 16)
            sp.wait_ge(none_ok, 1)
            sp.dma_start(s["src"].rearrange("(t p k) o -> p t (k o)", p=QT, k=K),
                         none[:].rearrange("p (t k) -> p t k", k=K)).then_inc(none_out, 16)
            def load_piece(i):
                n = PC if i < FULLP else LASTC
                sp.dma_start(raw[:, i % 2, :, 0:n], edge_v[:, :, i * PC:i * PC + n])\
                    .then_inc(raw_in[i % 2], 16)

            load_piece(0)
            load_piece(1)
            j = 0
            done = 0
            for b in range(B):
                for i in range(2):
                    dst = s["qk"[i]]
                    for m in range(2):
                        for c in range(NCH):
                            sp.wait_ge(p3_ok, j + 1)
                            sp.wait_ge(p2_ok, j + 1)
                            r0 = b * C + m * P
                            sp.dma_start(dst[:, r0:r0 + P, c * CH:(c + 1) * CH].rearrange("t p c -> p t c"),
                                         parts[:, j % 2]).then_inc(parts_out[j % 2], 16)
                            if i == 1 and c == 0:
                                sp.dma_start(dst[:, r0:r0 + P, NTOK:KPAD].rearrange("t p c -> p t c"),
                                             parts[:, j % 2, :, 0:KPAD - NTOK]).then_inc(parts_out[j % 2], 16)
                            j += 1
                            if (j * NPIECE) // (B * NP) > done:
                                sp.wait_ge(pay_ok, done + 1)
                                sp.dma_start(s["pay"][:, done * PC * 4:(done + 1) * PC * 4],
                                             pay[:, done % 2].rearrange("p c f -> p (c f)"))\
                                    .then_inc(pay_out[done % 2], 16)
                                if done + 2 <= FULLP:
                                    load_piece(done + 2)
                                done += 1
                sp.wait_ge(v_ok, KT * (b + 1))
                sp.dma_start(s["v"][b * HEADS:(b + 1) * HEADS].rearrange("h p n -> p h n"),
                             vrow[:].rearrange("p h t w -> p h (t w)")).then_inc(v_out, 16)
            sp.wait_ge(v_out, 16 * B)
            sp.wait_ge(none_out, 16)
            for i in range(2):
                sp.wait_ge(parts_out[i], 16 * (B * NP // 2 + (B * 2) // 2))
                sp.wait_ge(pay_out[i], 16 * (NPIECE // 2))

        @block.gpsimd
        def _(pool):
            pool.memset(identf[:], 0.0).then_inc(zeroed, 1)
            pool.memset(before[:], 1.0).then_inc(zeroed, 1)
            pool.memset(xT[:, :, NTOK:KPAD], 0.0).then_inc(const, 1)
            pool.wait_ge(zeroed, 2)
            pool.affine_select(out=identf[:], in_=identf[:], compare_op=ALU.not_equal, fill=1.0, base=0,
                               pattern=[[-1, P]], channel_multiplier=1).then_inc(const, 1)
            pool.affine_select(out=before[:], in_=before[:], compare_op=ALU.is_gt, fill=0.0, base=0,
                               pattern=[[1, P]], channel_multiplier=-1).then_inc(const, 1)
            for j in range(B * NP):
                pool.wait_ge(p1_ok, j + 1)
                if j >= 2:
                    pool.wait_ge(p2_ok, j - 1)
                pool.tensor_tensor(rest[:, j % 2], full[:, j % 2], parts[:, j % 2, 0], ALU.subtract)\
                    .then_inc(rest_ok, 1)
                pool.wait_ge(p2_ok, j + 1)
                pool.tensor_tensor(parts[:, j % 2, 2], rest[:, j % 2], parts[:, j % 2, 1], ALU.subtract)\
                    .then_inc(p3_ok, 1)

        @block.scalar
        def _(act):
            j = 0
            t = 0
            for b in range(B):
                for g in range(NG):
                    act.wait_ge(turned, t + 1)
                    if b == 1 and g == 0:
                        act.wait_ge(v_ps, KT)
                    h, c = g % 2, g // 2
                    act.activation(xT[:, h, c * CH:(c + 1) * CH], p_t[t % 2][:, 0:CH], ACT.Copy)\
                        .then_inc(xt_ok, 1)
                    t += 1
                for i in range(2):
                    for m in range(2):
                        for c in range(NCH):
                            act.wait_ge(proj, j + 1)
                            if j == 0:
                                act.wait_ge(w_in, 16 * 7)
                            if j >= 2:
                                act.wait_ge(p3_ok, j - 1)
                                act.wait_ge(rest_ok, j - 1)
                                pads = sum(1 for q in range(j - 1) if q % 2 == j % 2
                                           and (q // (2 * NCH)) % 2 == 1 and q % NCH == 0)
                                act.wait_ge(parts_out[j % 2], 16 * ((j - 2) // 2 + 1 + pads))
                            act.activation(full[:, j % 2], p_p[j % 2][:, 0:CH], ACT.Identity,
                                           bias=qkb[:, i, m:m + 1]).then_inc(full_ok, 1)
                            act.wait_ge(full_ok, j + 1)
                            act.activation(parts[:, j % 2, 0], full[:, j % 2], ACT.Copy).then_inc(p1_ok, 1)
                            act.wait_ge(rest_ok, j + 1)
                            act.activation(parts[:, j % 2, 1], rest[:, j % 2], ACT.Copy).then_inc(p2_ok, 1)
                            j += 1
                for kt in range(KT):
                    n = b * KT + kt
                    act.wait_ge(v_sum, n + 1)
                    if kt == 0 and b:
                        act.wait_ge(v_out, 16 * b)
                    act.activation(vrow[:, :, kt, 0:HD], vtmp[:, n % 2].rearrange("p (h d) -> p h d", d=HD),
                                   ACT.Copy, scale=wk[:, kt:kt + 1]).then_inc(v_ok, 1)

        @block.tensor
        def _(pe):
            pe.wait_ge(const, 3)
            t = j = 0

            def base(i):
                pe.wait_ge(sums_ok, i + 1)
                pe.matmul(p_b[:, 0:PG], before[:], sums[:], start=True, stop=True).then_inc(base_ok, 1)

            done = 0
            for b in range(B):
                pe.wait_ge(x_in[b], 16)
                for g in range(NG):
                    if t >= 2:
                        pe.wait_ge(xt_ok, t - 1)
                    h, c = g % 2, g // 2
                    for q in range(TPC):
                        ins = pe.transpose(p_t[t % 2][:, q * QT:(q + 1) * QT],
                                           xtok[:, b * tb + c * TPC + q, h * P:(h + 1) * P], identf[0:QT, 0:QT])
                    ins.then_inc(turned, 1)
                    t += 1
                pe.wait_ge(w_in, 16 * 7)
                for i in range(2):
                    for m in range(2):
                        for c in range(NCH):
                            pe.wait_ge(xt_ok, b * NG + 2 * c + 2)
                            if j >= 2:
                                pe.wait_ge(full_ok, j - 1)
                            for h in range(2):
                                ins = pe.matmul(p_p[j % 2][:, 0:CH], w[:, i, h, m * P:(m + 1) * P],
                                                xT[:, h, c * CH:(c + 1) * CH], start=(h == 0), stop=(h == 1))
                            ins.then_inc(proj, 1)
                            j += 1
                            if (j * NPIECE) // (B * NP) > done:
                                base(done)
                                done += 1
                for kt in range(KT):
                    n = b * KT + kt
                    if n >= 2:
                        pe.wait_ge(v_sum, n - 1)
                    for h in range(2):
                        ins = pe.matmul(p_v[n % 2][:, 0:C], xT[:, h, kt * P:(kt + 1) * P], w[:, 2, h, :],
                                        start=(h == 0), stop=(h == 1))
                    ins.then_inc(v_ps, 1)
            assert done == NPIECE

        @block.vector
        def _(dve):
            own_t = Tally(own)
            dve.memset(none[:], M).then_inc(none_ok, 1)
            own_t.inc(dve.memset(pos[:], 0.0))
            dve.wait_ge(w_in, 16 * 7)
            vsub = [0]

            def value_sums(upto):
                while vsub[0] < min(upto, B * KT):
                    n = vsub[0]
                    if n % KT == 0:
                        if n:
                            dve.wait_ge(v_out, 16)
                        for h in range(HEADS):
                            ins = dve.tensor_copy(vrow[:, h, :, HD], wk[:])
                        own_t.inc(ins)
                    dve.wait_ge(v_ps, n + 1)
                    if n >= 2:
                        dve.wait_ge(v_ok, n - 1)
                    dve.tensor_tensor(vtmp[:, n % 2], p_v[n % 2][:, 0:C], bvb[:], ALU.add).then_inc(v_sum, 1)
                    vsub[0] += 1

            def piece(i):
                r = raw[:, i % 2]
                src, dst = r[:, 0], r[:, 1]
                py = pay[:, i % 2]
                if i < FULLP:
                    dve.wait_ge(raw_in[i % 2], 16 * (i // 2 + 1))
                else:
                    own_t.inc(dve.memset(r[:, :, LASTC if i == FULLP else 0:PC], M))
                    if i == FULLP:
                        dve.wait_ge(raw_in[i % 2], 16 * (i // 2 + 1))
                    dve.wait_ge(own, own_t.value())
                if i >= 2:
                    dve.wait_ge(pay_out[i % 2], 16 * (i // 2))
                own_t.inc(dve.tensor_scalar(e1[:], dst, 1.0, None, ALU.add))
                own_t.inc(dve.tensor_scalar(eh[:], dst, 7, None, ALU.arith_shift_right))
                own_t.inc(dve.tensor_scalar(es[:], src, 0.0, float(M), ALU.is_lt, ALU.mult))
                dve.wait_ge(own, own_t.value())
                own_t.inc(dve.tensor_scalar(ev[:], e1[:], float(M), None, ALU.is_le))
                own_t.inc(dve.tensor_copy(py[:, :, 1], eh[:]))
                own_t.inc(dve.scalar_tensor_tensor(py[:, :, 0], eh[:], -float(P), e1[:], ALU.mult, ALU.add))
                own_t.inc(dve.tensor_tensor(es[:], es[:], src, ALU.add))
                dve.wait_ge(own, own_t.value())
                own_t.inc(dve.tensor_scalar(esi[:], es[:], 0.0, float(M - 1), ALU.max, ALU.min))
                own_t.inc(dve.scalar_tensor_tensor(ev[:], e1[:], 1.0, ev[:], ALU.is_ge, ALU.mult))
                dve.wait_ge(own, own_t.value())
                own_t.inc(dve.tensor_scalar(esh[:], esi[:], 7, None, ALU.arith_shift_right))
                ev3 = ev[:].rearrange("p (g c) -> p g c", c=GC)
                own_t.inc(dve.tensor_copy(pre[:, :, 0], ev3[:, :, 0]))
                for c in range(1, GC):
                    dve.wait_ge(own, own_t.value())
                    own_t.inc(dve.tensor_tensor(pre[:, :, c], pre[:, :, c - 1], ev3[:, :, c], ALU.add))
                dve.wait_ge(own, own_t.value())
                dve.tensor_copy(sums[:], pre[:, :, GC - 1]).then_inc(sums_ok, 1)
                own_t.inc(dve.tensor_copy(py[:, :, 3], esh[:]))
                dve.scalar_tensor_tensor(py[:, :, 2], esh[:], -float(P), esi[:], ALU.mult, ALU.add)\
                    .then_inc(pay_ok, 1)
                dve.wait_ge(base_ok, i + 1)
                own_t.inc(dve.tensor_tensor(pre[:], pre[:], p_b[:, 0:PG].unsqueeze(2).broadcast_to([P, PG, GC]),
                                            ALU.add))
                dve.wait_ge(own, own_t.value())
                own_t.inc(dve.tensor_tensor(pos[:, i * PC:(i + 1) * PC], pre[:].rearrange("p g c -> p (g c)"),
                                            ev[:], ALU.mult))
                dve.wait_ge(own, own_t.value())

            for i in range(NPIECE):
                piece(i)
                if (i + 1) * 2 % NPIECE == 0:
                    value_sums(KT * (i + 1) * 2 // NPIECE)


def attend(nc, a, s, xtok, pos):
    ctx = ExitStack()
    with ctx:
        def sb(name, shape, dt):
            return ctx.enter_context(nc.sbuf_tensor(name, shape, dt))

        def pb(name):
            return ctx.enter_context(nc.psum_tensor(name, [P, 512], F32))

        def sem(name):
            return ctx.enter_context(nc.semaphore(name))

        qa = sb("qa", [P, 2, NTOK], BF16)
        qb = sb("qb", [P, 2, NTOK], BF16)
        ka = sb("ka", [P, 2, KPAD], BF16)
        kb = sb("kb", [P, 2, KPAD], BF16)
        vv = sb("vv", [P, 2, KT, VW], F32)
        pay = sb("pay", [P, 2, NCH, ITC, 4], BF16)
        prob = sb("prob", [P, 4, CH], F32)
        osb = sb("osb", [P, CH], F32)
        part = sb("part", [QT, TPC, NCH], F32)
        mx = sb("mx", [QT, TPC], F32)
        fold = sb("fold", [P, VW], F32)
        identf = sb("identf", [P, P], F32)
        identb = sb("identb", [P, P], BF16)
        ones = sb("ones", [P, P], BF16)
        blocks = sb("blocks", [P, P], BF16)
        gamma = sb("gamma", [QT, 1], F32)
        rden = sb("rden", [QT, TPC], F32)
        gden = sb("gden", [QT, TPC], F32)
        delta = sb("delta", [QT, TPC, HD], F32)
        places = sb("places", [P, P, GC], BF16)
        count1 = sb("count1", [P, P], F32)
        countb = sb("countb", [P, DHI], F32)
        lane1 = sb("lane1", [P, 1], F32)
        turn = sb("turn", [P, 1], F32)
        earlier = sb("earlier", [P, P], F32)
        onehot = sb("onehot", [P, 2, P, GC], BF16)
        packed = sb("packed", [P, EPI, 4], F32)
        key = sb("key", [P, EPI], F32)
        diag = sb("diag", [P, 2, 2, P], BF16)
        lo_rows = sb("lo_rows", [P, 2, P], F32)
        lo_cols = sb("lo_cols", [P, 2, P], BF16)
        hi_cols = sb("hi_cols", [P, 2, DHI], BF16)
        same = sb("same", [P, P], F32)
        found = sb("found", [P, DHI], F32)
        local = sb("local", [P, EPI], F32)
        begin = sb("begin", [P, EPI], F32)
        seen = sb("seen", [P, DHI], F32)
        rank = sb("rank", [P, EPI], F32)
        over = sb("over", [P, EPI], F32)
        empty = sb("empty", [P, EPI], F32)
        where = sb("where", [P, EPI], I32)
        who = sb("who", [P, EPI], I32)
        ps_a = [pb("ps_a0"), pb("ps_a1")]
        ps_s = [pb("ps_s0"), pb("ps_s1")]
        ps_o = pb("ps_o")
        ps_m = pb("ps_m")
        ps_e = [pb("ps_e0"), pb("ps_e1")]

        zeroed = sem("zeroed1")
        const = sem("const1")
        init = sem("init1")
        gamma_in = sem("gamma_in")
        head_in = [sem(f"head_in{i}") for i in range(2)]
        lead = sem("lead")
        lead_max = sem("lead_max")
        mx_ok = sem("mx_ok")
        mrow = sem("mrow")
        mrow_ok = sem("mrow_ok")
        score = sem("score")
        prob_ok = sem("prob_ok")
        pv = sem("pv")
        osb_ok = sem("osb_ok")
        folded = sem("folded")
        fold_read = sem("fold_read")
        own = sem("own1")
        hot_ok = sem("hot_ok")
        edge_ps = sem("edge_ps")
        edge_read = sem("edge_read")
        diag_ok = sem("diag_ok")
        cols_ok = sem("cols_ok")
        where_ok = sem("where_ok")
        sent = sem("sent")
        paced = sem("paced")

        NL = TPC * NCH
        LSTEPS = 19
        lead_at = [range(NL * k // LSTEPS, NL * (k + 1) // LSTEPS) if k < LSTEPS else range(0)
                   for k in range(KT)]
        MSTEP = 21
        DMAS = 14
        pay_v = s["pay"].rearrange("p (h n) -> h p n", h=B * HEADS)

        def chunks(eng, body):
            with eng.Fori(0, B) as b:
                with eng.Fori(0, HEADS // 2) as hp:
                    pair = b * (HEADS // 2) + hp
                    for slot in range(2):
                        first = pair * (2 * NCH) + slot * NCH
                        with eng.Fori(0, NCH - 1) as c:
                            body(first + c, pair, b, hp * 2 + slot, slot, c, slot, c + 1)
                        body(first + (NCH - 1), pair, b, hp * 2 + slot, slot, NCH - 1, 1 - slot, 0)

        block = ctx.enter_context(nc.Block())

        @block.sync
        def _(sp):
            sp.dma_start(gamma[:], a["gamma"].partition_broadcast(QT)).then_inc(gamma_in, 16)

            def load(h, slot):
                rows = bass.ds(h * HD, HD)

                def get(dst, src):
                    sp.dma_start(dst, src).then_inc(head_in[slot], 16)
                for g, part_ in enumerate((0, 0, 1, 1)):
                    get(qa[g * HD:(g + 1) * HD, slot, :], s["q"][part_, rows, :])
                for g, part_ in enumerate((0, 2)):
                    get(qb[g * HD:(g + 1) * HD, slot, :], s["q"][part_, rows, :])
                for g, part_ in enumerate((0, 1, 0, 1)):
                    get(ka[g * HD:(g + 1) * HD, slot, :], s["k"][part_, rows, :])
                for g, part_ in enumerate((2, 0)):
                    get(kb[g * HD:(g + 1) * HD, slot, :], s["k"][part_, rows, :])
                get(vv[:, slot].rearrange("p t w -> p (t w)"), s["v"][bass.ds(h, 1)].rearrange("h p n -> p (h n)"))
                get(pay[:, slot].rearrange("p c e f -> p (c e f)"),
                    pay_v[bass.ds(h, 1)].rearrange("h p n -> p (h n)"))

            load(0, 0)
            load(1, 1)
            with sp.Fori(1, B * HEADS // 2) as pair:
                for slot in range(2):
                    sp.wait_ge(pv, (pair * 2 + slot - 1) * (NCH * KT))
                    load(pair * 2 + slot, slot)
            sp.wait_ge(pv, (B * HEADS - 1) * NCH * KT)
            load(0, 0)
            sp.wait_ge(head_in[0], 16 * DMAS * (B * HEADS // 2 + 1))

        @block.gpsimd
        def _(pool):
            for t in (identf, fold):
                pool.memset(t[:], 0.0).then_inc(zeroed, 1)
            pool.memset(earlier[:], 1.0).then_inc(zeroed, 1)
            pool.wait_ge(zeroed, 3)
            pool.affine_select(out=identf[:], in_=identf[:], compare_op=ALU.not_equal, fill=1.0, base=0,
                               pattern=[[-1, P]], channel_multiplier=1).then_inc(const, 1)
            pool.affine_select(out=earlier[:], in_=earlier[:], compare_op=ALU.is_gt, fill=0.0, base=0,
                               pattern=[[-1, P]], channel_multiplier=1).then_inc(const, 1)
            pool.affine_select(out=fold[:], in_=fold[:], compare_op=ALU.not_equal, fill=1.0, base=0,
                               pattern=[[-1, VW]], channel_multiplier=1).then_inc(zeroed, 1)
            pool.wait_ge(zeroed, 4)
            pool.affine_select(out=fold[:], in_=fold[:], compare_op=ALU.not_equal, fill=1.0, base=-64,
                               pattern=[[-1, VW]], channel_multiplier=1).then_inc(const, 1)
            pool.iota(places[:], [[1, P], [0, GC]], base=1, channel_multiplier=0,
                      allow_small_or_imprecise_dtypes=True).then_inc(const, 1)
            pool.iota(count1[:], [[1, P]], base=1, channel_multiplier=0,
                      allow_small_or_imprecise_dtypes=True).then_inc(const, 1)
            pool.iota(countb[:], [[1, DHI]], base=0, channel_multiplier=0,
                      allow_small_or_imprecise_dtypes=True).then_inc(const, 1)
            pool.iota(lane1[:], [[0, 1]], base=1, channel_multiplier=1,
                      allow_small_or_imprecise_dtypes=True).then_inc(const, 1)
            past = pool.to_reg(M * K - 1)
            with pool.Fori(0, NIT) as n:
                pool.wait_ge(where_ok, n + 1)
                pool.wait_ge(paced, n)
                pool.tensor_tensor(turn[:], lane1[:], lane1[:], ALU.add).then_inc(paced, 1)
                for e in range(EPI):
                    pool.indirect_dma_start(s["src"], bass.IndirectOffsetOnAxis(ap=where[:, e:e + 1].bitcast(U32), axis=0),
                                            who[:, e:e + 1], None, bounds_check=past, oob_is_err=False)\
                        .then_inc(sent, 16)
            pool.wait_ge(sent, 16 * EPI * NIT)

        @block.scalar
        def _(act):
            act.wait_ge(const, 7)
            act.wait_ge(init, 10)

            def body(n, pair, b, h, slot, c, nslot, nc_):
                for k in range(KT):
                    act.wait_ge(score, n * KT + (k + 1))
                    act.wait_ge(pv, n * KT + max(k - 3, 0))
                    act.activation(prob[:, k % 4], ps_s[k % 2][:, 0:CH], ACT.Exp).then_inc(prob_ok, 1)
                    if k % 2 and k // 2 < EPI:
                        e = k // 2
                        act.wait_ge(edge_read, n * SLOTS + (e + 1))
                        for f in range(2):
                            act.activation(diag[:, e % 2, f], identb[:], ACT.Copy, scale=packed[:, e, f:f + 1])\
                                .then_inc(diag_ok, 1)
                act.wait_ge(pv, n * KT + KT)
                act.wait_ge(folded, n + 1)
                act.activation(osb[:], ps_o[:, 0:CH], ACT.Copy).then_inc(osb_ok, 1)

            chunks(act, body)

        @block.tensor
        def _(pe):
            pe.wait_ge(const, 7)
            pe.wait_ge(init, 10)

            def leading(m, slot, c, js, first=False):
                for j in js:
                    q, kc = j // NCH, j % NCH
                    if not (first and j < 2):
                        pe.wait_ge(lead_max, m * NL + (j - 1) if j >= 1 else m * NL)
                    pe.matmul(ps_a[j % 2][0:QT, 0:CH], qa[:, slot, bass.ds(c * CH + q * QT, QT)],
                              ka[:, slot, kc * CH:(kc + 1) * CH], start=True, stop=True).then_inc(lead, 1)

            def max_rows(m):
                pe.wait_ge(mx_ok, m + 1)
                for q in range(TPC):
                    ins = pe.matmul(ps_m[:, q * QT:(q + 1) * QT], mx[:, q:q + 1].broadcast_to([QT, P]),
                                    identf[0:QT, 0:QT], start=True, stop=True)
                ins.then_inc(mrow, 1)

            def fold_heads(n):
                pe.wait_ge(osb_ok, n)
                for q in range(TPC):
                    ins = pe.matmul(ps_m[0:QT, q * VW:(q + 1) * VW], osb[:, q * QT:(q + 1) * QT], fold[:],
                                    start=True, stop=True)
                ins.then_inc(folded, 1)

            def edge_slot(n, slot, c, e):
                ps = ps_e[e % 2]
                pe.wait_ge(edge_read, n * SLOTS + e)
                if e < EPI:
                    pe.wait_ge(hot_ok, n * EPI + (e + 1))
                    for g in range(GC):
                        ins = pe.matmul(ps[:, 0:4], onehot[:, e % 2, :, g],
                                        pay[:, slot, bass.ds(c, 1), e * GC + g, :].rearrange("p c f -> p (c f)"),
                                        start=(g == 0), stop=(g == GC - 1))
                if 1 <= e <= EPI:
                    pe.wait_ge(diag_ok, (n * EPI + e) * 2)
                    d = diag[:, (e - 1) % 2]
                    pe.matmul(ps[:, 8:8 + P], ones[:], d[:, 0], start=True, stop=True)
                    pe.matmul(ps[:, 8 + P:8 + 2 * P], ones[:], d[:, 0], start=True, stop=False)
                    ins = pe.matmul(ps[:, 8 + P:8 + 2 * P], blocks[:], d[:, 1], start=False, stop=True)
                if e >= 2:
                    pe.wait_ge(cols_ok, n * EPI + (e - 1))
                    pe.matmul(ps[:, 272:272 + DHI], lo_rows[:, e % 2], seen[:], start=True, stop=True)
                    ins = pe.matmul(ps[:, 336:336 + DHI], lo_cols[:, e % 2], hi_cols[:, e % 2], start=True, stop=True)
                ins.then_inc(edge_ps, 1)

            def attend_values(n, slot, k):
                if k == 0:
                    pe.wait_ge(osb_ok, n)
                pe.wait_ge(prob_ok, n * KT + (k + 1))
                o = 64 * (k % 2)
                pe.matmul(ps_o[o:o + VW, 0:CH], vv[:, slot, k], prob[:, k % 4], start=(k < 2), stop=(k >= KT - 2),
                          skip_group_check=True).then_inc(pv, 1)

            pe.wait_ge(head_in[0], 16 * DMAS)
            leading(0, 0, 0, range(NL), first=True)
            max_rows(0)
            pe.wait_ge(head_in[1], 16 * DMAS)

            def body(n, pair, b, h, slot, c, nslot, nc_):
                for k in range(KT):
                    if k == 0:
                        pe.wait_ge(mrow_ok, n + 1)
                        pe.wait_ge(prob_ok, n * KT)
                    elif k == 1:
                        pe.wait_ge(prob_ok, n * KT)
                    else:
                        pe.wait_ge(prob_ok, n * KT + (k - 1))
                    ps = ps_s[k % 2][:, 0:CH]
                    qs = bass.ds(c * CH, CH)
                    pe.matmul(ps, ka[:, slot, k * P:(k + 1) * P], qa[:, slot, qs], start=True, stop=False)
                    pe.matmul(ps, kb[:, slot, k * P:(k + 1) * P], qb[:, slot, qs], start=False, stop=True)\
                        .then_inc(score, 1)
                    if k == 1:
                        fold_heads(n)
                    if k == 0 and nslot != slot:
                        pe.wait_ge(head_in[nslot], (pair + (1 + slot)) * (16 * DMAS))
                    leading(n + 1, nslot, nc_, lead_at[k])
                    if k == MSTEP:
                        pe.wait_ge(fold_read, n)
                        max_rows(n + 1)
                    if k % 2 == 0:
                        edge_slot(n, slot, c, k // 2)
                    if k >= 2:
                        attend_values(n, slot, k - 2)
                for k in (KT - 2, KT - 1):
                    attend_values(n, slot, k)

            chunks(pe, body)
            fold_heads(NIT)

        @block.vector
        def _(dve):
            dve.memset(osb[:], 0.0).then_inc(init, 1)
            dve.memset(ones[:], 1.0).then_inc(init, 1)
            dve.memset(blocks[:], float(P)).then_inc(init, 1)
            dve.memset(seen[:], 0.0).then_inc(init, 1)
            dve.memset(ps_o[:], 0.0).then_inc(init, 1)
            dve.memset(kb[64:P, :, :], 0.0).then_inc(init, 1)
            dve.memset(qb[64:P, :, :], 0.0).then_inc(init, 1)
            dve.wait_ge(init, 7)
            dve.memset(kb[64:65, :, :], -1.0).then_inc(init, 1)
            dve.memset(kb[96:97, :, :], -1.0).then_inc(init, 1)
            dve.wait_ge(const, 7)
            dve.tensor_copy(identb[:], identf[:]).then_inc(init, 1)
            dve.wait_ge(init, 10)

            def places_of(col, e):
                dve.tensor_tensor(onehot[:, e % 2], pos[:, col].unsqueeze(1).broadcast_to([P, P, GC]), places[:],
                                  ALU.is_equal).then_inc(hot_ok, 1)

            def maxima(m, js):
                for j in js:
                    q, kc = j // NCH, j % NCH
                    dve.wait_ge(lead, m * NL + (j + 1))
                    dve.tensor_reduce(part[:, q, kc:kc + 1], ps_a[j % 2][0:QT, 0:CH], AX.X, ALU.max)\
                        .then_inc(lead_max, 1)

            def max_of_parts(m):
                dve.wait_ge(lead_max, (m + 1) * NL)
                if not isinstance(m, int):
                    dve.wait_ge(mrow, m)
                dve.tensor_reduce(mx[:], part[:], AX.X, ALU.max).then_inc(mx_ok, 1)

            def max_parts(own_t, m, slot, c):
                cs = bass.ds(c * CH, CH)
                dve.wait_ge(mrow, m + 1)
                own_t.inc(dve.tensor_copy(qb[64:P, slot, cs], ps_m[64:P, 0:CH]))
                dve.wait_ge(own, own_t.value())
                dve.tensor_tensor(qb[96:P, slot, cs], ps_m[96:P, 0:CH], qb[96:P, slot, cs], ALU.subtract)\
                    .then_inc(mrow_ok, 1)

            def edge_slot(own_t, n, e):
                ps = ps_e[e % 2]
                dve.wait_ge(edge_ps, n * SLOTS + (e + 1))
                dve.wait_ge(edge_read, n * SLOTS + e)
                dve.wait_ge(own, own_t.value())
                if e >= 2:
                    dve.wait_ge(cols_ok, n * EPI + (e - 1))
                if e < EPI:
                    ins = dve.tensor_copy(packed[:, e], ps[:, 0:4])
                if 1 <= e <= EPI:
                    f = e - 1
                    dve.tensor_scalar(lo_rows[:, f % 2], ps[:, 8:8 + P], lane1[:, 0:1], None, ALU.is_equal)
                    ins = dve.scalar_tensor_tensor(same[:], ps[:, 8 + P:8 + 2 * P], key[:, f:f + 1], earlier[:],
                                                   ALU.is_equal, ALU.mult, accum_out=local[:, f:f + 1])
                if e >= 2:
                    f = e - 2
                    dve.tensor_tensor_reduce(found[:], ps[:, 272:272 + DHI], hi_cols[:, f % 2], 1.0, 0.0,
                                             ALU.mult, ALU.add, begin[:, f:f + 1])
                    ins = dve.tensor_tensor(seen[:], seen[:], ps[:, 336:336 + DHI], ALU.add)
                ins.then_inc(edge_read, 1)
                if e < EPI:
                    dve.wait_ge(edge_read, n * SLOTS + (e + 1))
                    own_t.inc(dve.scalar_tensor_tensor(key[:, e:e + 1], packed[:, e, 1:2], float(P), packed[:, e, 0:1],
                                                       ALU.mult, ALU.add))
                    dve.tensor_scalar(lo_cols[:, e % 2], count1[:], packed[:, e, 0:1], None, ALU.is_equal)
                    dve.tensor_scalar(hi_cols[:, e % 2], countb[:], packed[:, e, 1:2], None, ALU.is_equal)\
                        .then_inc(cols_ok, 1)
                if e + 2 < EPI:
                    places_of(bass.ds(n * ITC + (e + 2) * GC, GC), e + 2)
                elif e >= EPI:
                    places_of(bass.ds((n + 1) * ITC + (e - EPI) * GC, GC), e - EPI)

            def place_edges(own_t, n):
                dve.wait_ge(edge_read, (n + 1) * SLOTS)
                dve.wait_ge(own, own_t.value())
                own_t.inc(dve.tensor_tensor(rank[:], local[:], begin[:], ALU.add))
                own_t.inc(dve.tensor_scalar(empty[:], key[:], 1.0, BIG, ALU.is_lt, ALU.mult))
                dve.wait_ge(sent, n * (16 * EPI))
                dve.wait_ge(own, own_t.value())
                own_t.inc(dve.tensor_scalar(over[:], rank[:], float(K), BIG, ALU.is_ge, ALU.mult))
                own_t.inc(dve.scalar_tensor_tensor(rank[:], key[:], float(K), rank[:], ALU.mult, ALU.add))
                own_t.inc(dve.scalar_tensor_tensor(who[:], packed[:, :, 3], float(P), packed[:, :, 2], ALU.mult, ALU.add))
                dve.wait_ge(own, own_t.value())
                own_t.inc(dve.scalar_tensor_tensor(rank[:], rank[:], -float(K), empty[:], ALU.add, ALU.add))
                dve.wait_ge(own, own_t.value())
                dve.tensor_tensor(where[:], rank[:], over[:], ALU.add).then_inc(where_ok, 1)

            def add_head(own_t, n, b, h, c):
                dve.wait_ge(folded, n + 2)
                ps = ps_m[0:QT, 0:TPC * VW].rearrange("p (t w) -> p t w", w=VW)
                own_t.inc(dve.reciprocal(rden[:], ps[:, :, HD]))
                dve.wait_ge(own, own_t.value())
                own_t.inc(dve.tensor_scalar(gden[:], rden[:], gamma[:, 0:1], None, ALU.mult))
                dve.wait_ge(own, own_t.value())
                dve.tensor_tensor(delta[:], ps[:, :, 0:HD], gden[:].unsqueeze(2).broadcast_to([QT, TPC, HD]), ALU.mult)\
                    .then_inc(fold_read, 1)
                dve.wait_ge(fold_read, n + 1)
                dst = xtok[:, bass.ds(b * (TILES // B) + c * TPC, TPC), bass.ds(h * HD, HD)]
                own_t.inc(dve.tensor_tensor(dst, dst, delta[:], ALU.add))

            first = Tally(own)
            places_of(slice(0, GC), 0)
            places_of(slice(GC, 2 * GC), 1)
            maxima(0, range(NL))
            max_of_parts(0)
            max_parts(first, 0, 0, 0)
            dve.wait_ge(gamma_in, 16)
            OWN = EPI + 1 + 6 + 3

            def body(n, pair, b, h, slot, c, nslot, nc_):
                own_t = Tally(own, n * OWN + first.k)
                for k in range(KT):
                    maxima(n + 1, lead_at[k])
                    if k == LSTEPS:
                        max_of_parts(n + 1)
                    if k % 2 == 0:
                        edge_slot(own_t, n, k // 2)
                    if k == MSTEP:
                        max_parts(own_t, n + 1, nslot, nc_)
                place_edges(own_t, n)
                add_head(own_t, n, b, h, c)
                assert own_t.k == OWN, own_t.k

            chunks(dve, body)


def mix(nc, a, s, xtok, xhT, nodes):
    ctx = ExitStack()
    with ctx:
        def sb(name, shape, dt=F32):
            return ctx.enter_context(nc.sbuf_tensor(name, shape, dt))

        def pb(name):
            return ctx.enter_context(nc.psum_tensor(name, [P, 512], F32))

        def sem(name):
            return ctx.enter_context(nc.semaphore(name))

        w = sb("w1", [P, 3, 2, C])
        wT = sb("wT", [P, 2, 3, C])
        wb = sb("w1b", [QT, 3, C])
        wg = sb("wg", [P, 2, GF])
        att = sb("att", [QT, 2, GF])
        ident = sb("ident1", [P, P])
        stats = sb("stats", [QT, 4, nc.vector.BN_STATS_DIM])
        mv = sb("mv", [QT, TILES, 2])
        eps = sb("eps", [QT, 1])
        rstd = sb("rstd", [QT, TILES])
        shift = sb("shift", [QT, TILES])
        xn = sb("xn", [QT, 2, 2, C])
        xnT = sb("xnT", [P, 2, 4, QT])
        qk = sb("qk", [QT, 2, 2, 2, C])
        v = sb("v", [QT, 2, 2, C])
        dots = sb("dots", [QT, C])
        score = sb("score", [QT, 2, 2])
        top = sb("top", [QT, 2])
        wexp = sb("wexp", [QT, 2, 2])
        wsum = sb("wsum", [QT, 2])
        prod = sb("prod1", [QT, TILES, GF])
        last = sb("last", [1, ROW])
        ps_t = [pb("ps_t0"), pb("ps_t1")]
        ps_qk = [pb("ps_qk0"), pb("ps_qk1")]
        ps_v = [pb("ps_v0"), pb("ps_v1")]

        w_in = sem("w1_in")
        const = sem("const2")
        wturn = sem("wturn")
        wT_ok = sem("wT_ok")
        own = sem("own2")
        mv_ok = sem("mv_ok")
        var_ok = sem("var_ok")
        root_ok = sem("root_ok")
        norm_ok = sem("norm_ok")
        xn_ok = sem("xn_ok")
        turned = sem("turned1")
        xnT_ok = sem("xnT_ok")
        qk_ps = sem("qk_ps")
        v_ps = sem("v1_ps")
        qk_ok = sem("qk_ok")
        v_ok = sem("v1_ok")
        shifted = sem("shifted")
        exp_ok = sem("exp1_ok")
        mixed = sem("mixed")
        feat = sem("feat")
        feat_ok = sem("feat_ok")
        node_ok = sem("node_ok")
        node_out = sem("node_out")
        HT = TILES // B
        block = ctx.enter_context(nc.Block())

        @block.sync
        def _(sp):
            for i, n in enumerate(("Wq1", "Wk1", "Wv1")):
                sp.dma_start(w[:, i], a[n].rearrange("(t p) f -> p t f", p=P)).then_inc(w_in, 16)
            for i, n in enumerate(("bq1", "bk1", "bv1")):
                sp.dma_start(wb[:, i], a[n].partition_broadcast(QT)).then_inc(w_in, 16)
            sp.dma_start(wg[:], a["Wgat"].rearrange("(t p) f -> p t f", p=P)).then_inc(w_in, 16)
            for i, n in enumerate(("att_src", "att_dst")):
                sp.dma_start(att[:, i], a[n].rearrange("h e -> (h e)").partition_broadcast(QT)).then_inc(w_in, 16)
            sp.wait_ge(node_ok, 2)
            sp.dma_start(s["node"][0:M].rearrange("(t p) r -> p t r", p=QT), nodes[:]).then_inc(node_out, 16)
            sp.dma_start(s["node"][M:M + 1], last[:]).then_inc(node_out, 16)
            sp.wait_ge(node_out, 32)

        @block.gpsimd
        def _(pool):
            pool.memset(ident[:], 0.0).then_inc(const, 1)
            pool.memset(last[:, 0:GF], 0.0).then_inc(const, 1)
            pool.memset(last[:, GF:GF + GH], -1.0e30).then_inc(const, 1)
            pool.memset(last[:, GF + GH:ROW], 0.0).then_inc(const, 1)
            pool.memset(eps[:], LN_EPS).then_inc(const, 1)
            pool.wait_ge(const, 5)
            pool.affine_select(out=ident[:], in_=ident[:], compare_op=ALU.not_equal, fill=1.0, base=0,
                               pattern=[[-1, P]], channel_multiplier=1).then_inc(const, 1)

            def normed(dst, t):
                return pool.tensor_scalar(dst, xtok[:, t, :], rstd[:, t:t + 1], shift[:, t:t + 1], ALU.mult, ALU.add)

            pool.wait_ge(norm_ok, 1)
            for t in range(HT):
                if t >= 2:
                    pool.wait_ge(turned, t - 1)
                for img in range(2):
                    ins = normed(xn[:, t % 2, img], t + img * HT)
                ins.then_inc(xn_ok, 1)
            pool.wait_ge(norm_ok, 2)
            for t in range(TILES):
                pool.wait_ge(turned, HT + t - 1)
                normed(xn[:, t % 2, 0], t).then_inc(xn_ok, 1)

        @block.scalar
        def _(act):
            for i in range(3):
                act.wait_ge(wturn, i + 1)
                act.activation(wT[:, :, i, :],
                               ps_t[i % 2][:, 0:512].rearrange("p (h n) -> p h n", h=2), ACT.Copy)\
                    .then_inc(wT_ok, 1)
            act.wait_ge(const, 6)
            act.wait_ge(var_ok, 1)
            act.activation(rstd[:], mv[:, :, 1], ACT.Sqrt, bias=eps[:, 0:1]).then_inc(root_ok, 1)
            with act.Fori(0, HT // 2) as i:
                for par in range(2):
                    n = i * 2 + par
                    act.wait_ge(turned, n + 1)
                    act.wait_ge(v_ps, i * 2)
                    act.activation(xnT[:, par].rearrange("p b q -> p (b q)"), ps_t[par][:, 0:4 * QT], ACT.Copy)\
                        .then_inc(xnT_ok, 1)
                    act.wait_ge(shifted, n + 1)
                    act.activation(wexp[:], score[:], ACT.Exp).then_inc(exp_ok, 1)
            act.wait_ge(var_ok, 2)
            act.activation(rstd[:], mv[:, :, 1], ACT.Sqrt, bias=eps[:, 0:1]).then_inc(root_ok, 1)
            with act.Fori(0, HT) as i:
                for par in range(2):
                    n = i * 2 + par
                    act.wait_ge(turned, n + (HT + 1))
                    act.wait_ge(feat, i * 2)
                    src = ps_t[par][:, 0:2 * QT].rearrange("p (h q) -> p h q", h=2)
                    act.activation(xnT[:, par, 0:2], src, ACT.Copy).then_inc(xnT_ok, 1)
                    act.activation(xhT[:, :, bass.ds(n * QT, QT)], src, ACT.Copy).then_inc(xnT_ok, 1)

        @block.tensor
        def _(pe):
            pe.wait_ge(const, 6)
            pe.wait_ge(w_in, 16 * 9)
            for i in range(3):
                if i == 2:
                    pe.wait_ge(wT_ok, 1)
                for h in range(2):
                    for g in range(2):
                        ins = pe.transpose(ps_t[i % 2][:, h * C + g * P:h * C + (g + 1) * P],
                                           w[:, i, g, h * P:(h + 1) * P], ident[:])
                ins.then_inc(wturn, 1)
            pe.wait_ge(wT_ok, 3)
            with pe.Fori(0, HT // 2) as i:
                for par in range(2):
                    n = i * 2 + par
                    pe.wait_ge(xn_ok, n + 1)
                    pe.wait_ge(xnT_ok, i * 2 + (par - 1 if par else 0))
                    for img in range(2):
                        for h in range(2):
                            j = img * 2 + h
                            ins = pe.transpose(ps_t[par][:, j * QT:(j + 1) * QT], xn[:, par, img, h * P:(h + 1) * P],
                                               ident[0:QT, 0:QT])
                    ins.then_inc(turned, 1)
                    pe.wait_ge(xnT_ok, n + 1)
                    for img in range(2):
                        pe.wait_ge(qk_ok, n * 2)
                        for h in range(2):
                            ins = pe.matmul(ps_qk[img][0:QT, 0:2 * C], xnT[:, par, img * 2 + h],
                                            wT[:, h, 0:2].rearrange("p i n -> p (i n)"), start=(h == 0), stop=(h == 1))
                        ins.then_inc(qk_ps, 1)
                    pe.wait_ge(v_ok, i * 2)
                    for img in range(2):
                        for h in range(2):
                            ins = pe.matmul(ps_v[par][0:QT, img * C:(img + 1) * C], xnT[:, par, img * 2 + h],
                                            wT[:, h, 2], start=(h == 0), stop=(h == 1))
                    ins.then_inc(v_ps, 1)
            with pe.Fori(0, HT) as i:
                for par in range(2):
                    n = i * 2 + par
                    pe.wait_ge(xn_ok, n + (HT + 1))
                    pe.wait_ge(xnT_ok, i * 4 + HT)
                    for h in range(2):
                        ins = pe.transpose(ps_t[par][:, h * QT:(h + 1) * QT], xn[:, par, 0, h * P:(h + 1) * P],
                                           ident[0:QT, 0:QT])
                    ins.then_inc(turned, 1)
                    pe.wait_ge(xnT_ok, n * 2 + (HT + 1))
                    pe.wait_ge(feat_ok, i * 2)
                    for h in range(2):
                        ins = pe.matmul(ps_qk[par][0:QT, 0:GF], xnT[:, par, h], wg[:, h], start=(h == 0), stop=(h == 1))
                    ins.then_inc(feat, 1)

        @block.vector
        def _(dve):
            def moments(base, k):
                for t in range(0, TILES, 4):
                    dve.wait_ge(mv_ok, (k - 1) * TILES + t)
                    for q in range(4):
                        dve.bn_stats(stats[:, q], xtok[:, t + q, :]).then_inc(own, 1)
                    dve.wait_ge(own, base + t + 4)
                    for q in range(4):
                        dve.bn_aggr(mv[:, t + q, :], stats[:, q]).then_inc(mv_ok, 1)
                dve.wait_ge(mv_ok, k * TILES)
                dve.memset(stats[:, 0, 0:1], 0.0).then_inc(var_ok, 1)

            def scales(base, k):
                dve.wait_ge(root_ok, k)
                dve.reciprocal(rstd[:], rstd[:]).then_inc(own, 1)
                dve.wait_ge(own, base + 1)
                dve.scalar_tensor_tensor(shift[:], mv[:, :, 0], -1.0, rstd[:], ALU.mult, ALU.mult).then_inc(norm_ok, 1)

            moments(0, 1)
            scales(TILES, 1)
            base = TILES + 1
            STEPS = 2 * 2 + 3
            dve.wait_ge(w_in, 16 * 9)
            with dve.Fori(0, HT // 2) as i:
                for par in range(2):
                    n = i * 2 + par
                    t = Tally(own, n * STEPS + base)
                    for img in range(2):
                        dve.wait_ge(qk_ps, n * 2 + (img + 1))
                        dve.tensor_tensor(qk[:, par, img].rearrange("p i n -> p (i n)"), ps_qk[img][0:QT, 0:2 * C],
                                          wb[:, 0:2].rearrange("p i n -> p (i n)"), ALU.add).then_inc(qk_ok, 1)
                    dve.wait_ge(v_ps, n + 1)
                    dve.tensor_tensor(v[:, par], ps_v[par][0:QT, 0:2 * C].rearrange("p (b n) -> p b n", b=2),
                                      wb[:, 2:3].broadcast_to([QT, 2, C]), ALU.add).then_inc(v_ok, 1)
                    dve.wait_ge(qk_ok, n * 2 + 2)
                    for q in range(2):
                        for k in range(2):
                            dve.wait_ge(own, t.value())
                            t.inc(dve.tensor_tensor_reduce(dots[:], qk[:, par, q, 0], qk[:, par, k, 1], C ** -0.5, 0.0,
                                                           ALU.mult, ALU.add, score[:, q, k:k + 1]))
                    dve.wait_ge(own, t.value())
                    t.inc(dve.tensor_reduce(top[:], score[:], AX.X, ALU.max))
                    dve.wait_ge(own, t.value())
                    dve.tensor_tensor(score[:], score[:], top[:].unsqueeze(2).broadcast_to([QT, 2, 2]), ALU.subtract)\
                        .then_inc(shifted, 1)
                    dve.wait_ge(exp_ok, n + 1)
                    t.inc(dve.tensor_reduce(wsum[:], wexp[:], AX.X, ALU.add))
                    dve.wait_ge(own, t.value())
                    t.inc(dve.reciprocal(wsum[:], wsum[:]))
                    dve.wait_ge(own, t.value())
                    dve.tensor_tensor(wexp[:], wexp[:], wsum[:].unsqueeze(2).broadcast_to([QT, 2, 2]), ALU.mult)\
                        .then_inc(mixed, 1)
                    dve.wait_ge(mixed, n * 3 + 1)
                    dve.wait_ge(v_ok, n + 1)
                    for k in range(2):
                        for q in range(2):
                            dst = xtok[:, bass.ds(n + q * HT, 1), :].rearrange("p t c -> p (t c)")
                            ins = dve.scalar_tensor_tensor(dst, v[:, par, k], wexp[:, q, k:k + 1], dst, ALU.mult, ALU.add)
                        ins.then_inc(mixed, 1)
                        dve.wait_ge(mixed, n * 3 + (k + 2))
            base += HT * STEPS
            moments(base, 2)
            base += TILES
            scales(base, 2)
            base += 1
            with dve.Fori(0, HT) as i:
                for par in range(2):
                    n = i * 2 + par
                    dve.wait_ge(feat, n + 1)
                    dve.tensor_copy(nodes[:, bass.ds(n, 1), 0:GF].rearrange("p t f -> p (t f)"), ps_qk[par][0:QT, 0:GF])\
                        .then_inc(feat_ok, 1)
            dve.wait_ge(feat_ok, TILES)
            for i in range(2):
                dve.tensor_tensor(prod[:], nodes[:, :, 0:GF], att[:, i:i + 1].broadcast_to([QT, TILES, GF]), ALU.mult)\
                    .then_inc(own, 1)
                dve.wait_ge(own, base + i + 1)
                for h in range(GH):
                    ins = dve.tensor_reduce(nodes[:, :, GF + i * GH + h], prod[:, :, h * GE:(h + 1) * GE], AX.X, ALU.add)
                ins.then_inc(node_ok, 1)
                dve.wait_ge(node_ok, i + 1)


def route(nc, a, s, xtok, xhT, nodes, out):
    ctx = ExitStack()
    with ctx:
        def sb(name, shape, dt=F32):
            return ctx.enter_context(nc.sbuf_tensor(name, shape, dt))

        def pb(name, banks=1):
            return ctx.enter_context(nc.psum_tensor(name, [P, banks, 512], F32))

        def sem(name):
            return ctx.enter_context(nc.semaphore(name))

        KS = K + 1
        w1 = sb("we1", [P, GE, 2, FF])
        w2 = sb("we2", [P, GE, FF // P, C])
        b1 = sb("be1", [P, GE, FF // P])
        b2 = sb("be2", [QT, GE, C])
        bg = sb("bg", [QT, 3, GF])
        eps = sb("eps2", [QT, 1])
        turn = sb("turn2", [QT, 1])
        idx = sb("idx", [QT, 2, K], I32)
        rows = sb("rows", [QT, 2, KS, ROW])
        z = sb("z", [QT, GH, KS])
        zmax = sb("zmax", [QT, GH])
        wz = sb("wz", [QT, 2, GH, KS])
        den = sb("den", [QT, GH])
        prod = sb("prod", [QT, GF, KS])
        agg = sb("agg", [QT, TPC, GF])
        g16 = sb("g16", [QT, TPC, GF])
        mean = sb("mean", [QT, TPC])
        var = sb("var", [QT, TPC])
        sc = sb("sc", [QT, TPC, GE])
        beat = sb("beat", [QT, TPC, GE])
        cmp = sb("cmp", [QT, TPC, 1])
        gate = sb("gate", [QT, TPC, GE])
        gsum = sb("gsum", [QT, TPC])
        hid = sb("hid", [P, 2, FF // P, CH])
        ps_h = [pb("ps_h0"), pb("ps_h1")]
        ps_y = [pb("ps_y0", 2), pb("ps_y1", 2)]

        w_in = sem("w2_in")
        eps_ok = sem("eps_ok")
        idx_in = [sem(f"idx_in{i}") for i in range(2)]
        rows_in = [sem(f"rows_in{i}") for i in range(2)]
        rows_used = sem("rows_used")
        own = sem("own3")
        shifted = sem("shifted2")
        exp_ok = sem("exp2_ok")
        var_ok = sem("var2_ok")
        root_ok = sem("root2_ok")
        sc_ok = sem("sc_ok")
        gexp_ok = sem("gexp_ok")
        hid_ps = sem("hid_ps")
        hid_ok = sem("hid_ok")
        y_ps = sem("y_ps")
        y_read = sem("y_read")
        chunk_ok = sem("chunk_ok")
        out_ok = sem("out_ok")
        paced = sem("paced2")
        NF = FF // P
        src_v = s["src"].rearrange("(t p k) o -> t p (k o)", p=QT, k=K)
        out_v = out.rearrange("b h w c -> (b h w) c").rearrange("(t p) c -> p t c", p=QT)
        block = ctx.enter_context(nc.Block())

        @block.sync
        def _(sp):
            sp.dma_start(w1[:], a["W1"].rearrange("e (t p) f -> p e t f", p=P)).then_inc(w_in, 16)
            sp.dma_start(w2[:], a["W2"].rearrange("e (t p) c -> p e t c", p=P)).then_inc(w_in, 16)
            sp.dma_start(b1[:], a["b1"].rearrange("e (t p) -> p e t", p=P), allow_slow_non_contiguous=True)\
                .then_inc(w_in, 16)
            sp.dma_start(b2[:], a["b2"].rearrange("e c -> (e c)").partition_broadcast(QT)
                         .rearrange("p (e c) -> p e c", e=GE)).then_inc(w_in, 16)
            for i, n in enumerate(("b_gat", "ln_gamma", "ln_beta")):
                sp.dma_start(bg[:, i], a[n].partition_broadcast(QT)).then_inc(w_in, 16)
            for par in range(2):
                sp.dma_start(idx[:, par], src_v[par]).then_inc(idx_in[par], 16)
            with sp.Fori(1, TILES // 2) as i:
                for par in range(2):
                    sp.wait_ge(rows_in[par], i * (16 * K))
                    sp.dma_start(idx[:, par], src_v[bass.ds(i * 2 + par, 1)].rearrange("t p k -> p (t k)"))\
                        .then_inc(idx_in[par], 16)
            with sp.Fori(0, NCH * B) as c:
                sp.wait_ge(chunk_ok, c + 1)
                ts = bass.ds(c * TPC, TPC)
                sp.dma_start(out_v[:, ts, :], xtok[:, ts, :]).then_inc(out_ok, 16)
            sp.wait_ge(out_ok, 16 * NCH * B)

        @block.gpsimd
        def _(pool):
            pool.memset(eps[:], LN_EPS).then_inc(eps_ok, 1)
            pool.wait_ge(eps_ok, 1)
            with pool.Fori(0, TILES // 2) as i:
                for par in range(2):
                    pool.wait_ge(idx_in[par], i * 16 + 16)
                    pool.wait_ge(rows_used, i * 2)
                    pool.wait_ge(paced, i * 2 + par)
                    pool.tensor_tensor(turn[:], eps[:], eps[:], ALU.add).then_inc(paced, 1)
                    for k in range(K):
                        pool.indirect_dma_start(rows[:, par, k, :], None, s["node"],
                                                bass.IndirectOffsetOnAxis(ap=idx[:, par, k:k + 1].bitcast(U32), axis=0))\
                            .then_inc(rows_in[par], 16)

        @block.scalar
        def _(act):
            act.wait_ge(w_in, 16 * 7)
            act.wait_ge(eps_ok, 1)

            def hidden(c, e):
                for f in range(NF):
                    j = e * NF + f
                    act.wait_ge(hid_ps, c * (GE * NF) + (j + 1))
                    if f == 0:
                        act.wait_ge(y_ps, c * GE + (e - 1 if e >= 1 else 0))
                    act.activation(hid[:, e % 2, f], ps_h[j % 2][:, 0, 0:CH], ACT.Gelu, bias=b1[:, e, f:f + 1])\
                        .then_inc(hid_ok, 1)

            def gat(c, experts):
                for q in range(TPC):
                    if experts:
                        for e in ((0, 1), (2,), (3,), ())[q]:
                            hidden(c - 1, e)
                    act.wait_ge(shifted, c * TPC + (q + 1))
                    act.activation(wz[:, q % 2], z[:], ACT.Exp).then_inc(exp_ok, 1)
                act.wait_ge(var_ok, c + 1)
                act.activation(var[:], var[:], ACT.Sqrt, scale=1.0 / GF, bias=eps[:, 0:1]).then_inc(root_ok, 1)
                act.wait_ge(sc_ok, c + 1)
                act.activation(gate[:], sc[:], ACT.Exp).then_inc(gexp_ok, 1)

            gat(0, False)
            with act.Fori(1, NCH * B) as c:
                gat(c, True)
            for e in range(GE):
                hidden(NCH * B - 1, e)

        @block.tensor
        def _(pe):
            pe.wait_ge(w_in, 16 * 7)
            with pe.Fori(0, NCH * B) as c:
                def up(e):
                    for f in range(NF):
                        j = e * NF + f
                        pe.wait_ge(hid_ok, c * (GE * NF) + (j - 1 if j >= 1 else 0))
                        for h in range(2):
                            ins = pe.matmul(ps_h[j % 2][:, 0, 0:CH], w1[:, e, h, f * P:(f + 1) * P],
                                            xhT[:, h, bass.ds(c * CH, CH)], start=(h == 0), stop=(h == 1))
                        ins.then_inc(hid_ps, 1)

                def down(e):
                    pe.wait_ge(hid_ok, c * (GE * NF) + (e + 1) * NF)
                    pe.wait_ge(y_read, c * GE + (e - 1 if e >= 1 else 0))
                    for q in range(TPC):
                        for f in range(NF):
                            ins = pe.matmul(ps_y[e % 2][0:QT, q // 2, (q % 2) * C:(q % 2 + 1) * C],
                                            hid[:, e % 2, f, q * QT:(q + 1) * QT], w2[:, e, f],
                                            start=(f == 0), stop=(f == NF - 1))
                    ins.then_inc(y_ps, 1)

                up(0)
                for e in range(GE):
                    if e + 1 < GE:
                        up(e + 1)
                    down(e)

        @block.vector
        def _(dve):
            dve.wait_ge(w_in, 16 * 7)

            def experts(own_t, c, e):
                ts = [xtok[:, bass.ds(c * TPC + q, 1), :].rearrange("p t c -> p (t c)") for q in range(TPC)]
                dve.wait_ge(own, own_t.value())
                for q in range(TPC):
                    ins = dve.scalar_tensor_tensor(ts[q], b2[:, e], gate[:, q, e:e + 1], ts[q], ALU.mult, ALU.add)
                own_t.inc(ins)
                dve.wait_ge(y_ps, c * GE + (e + 1))
                dve.wait_ge(own, own_t.value())
                for q in range(TPC):
                    ins = dve.scalar_tensor_tensor(ts[q], ps_y[e % 2][0:QT, q // 2, (q % 2) * C:(q % 2 + 1) * C],
                                                   gate[:, q, e:e + 1], ts[q], ALU.mult, ALU.add)
                ins.then_inc(y_read, 1)
                dve.wait_ge(y_read, c * GE + (e + 1))
                if e == GE - 1:
                    own_t.inc(dve.tensor_copy(gsum[:], gate[:, :, 0]))
                    dve.wait_ge(own, own_t.value())
                    dve.tensor_copy(mean[:], gate[:, :, 0]).then_inc(chunk_ok, 1)
                    dve.wait_ge(chunk_ok, c + 1)

            def step(own_t, ins):
                own_t.inc(ins)
                dve.wait_ge(own, own_t.value())

            def node_tile(own_t, c, q, i, par):
                r = rows[:, par]
                t = c * TPC + q
                mine = nodes[:, bass.ds(t, 1), :].rearrange("p t r -> p (t r)")
                own_t.inc(dve.tensor_copy(r[:, K, :], mine))
                dve.wait_ge(rows_in[par], (i + 1) * (16 * K))
                dve.wait_ge(own, own_t.value())
                step(own_t, dve.tensor_tensor(z[:], r[:, :, GF:GF + GH].rearrange("p k h -> p h k"),
                                              mine[:, GF + GH:ROW].unsqueeze(2).broadcast_to([QT, GH, KS]), ALU.add))
                step(own_t, dve.scalar_tensor_tensor(z[:], z[:], 0.2, z[:], ALU.mult, ALU.max))
                step(own_t, dve.tensor_reduce(zmax[:], z[:], AX.X, ALU.max))
                dve.tensor_tensor(z[:], z[:], zmax[:].unsqueeze(2).broadcast_to([QT, GH, KS]), ALU.subtract)\
                    .then_inc(shifted, 1)
                dve.wait_ge(exp_ok, c * TPC + (q + 1))
                wq = wz[:, q % 2]
                own_t.inc(dve.tensor_reduce(den[:], wq, AX.X, ALU.add))
                for h in range(GH):
                    ins = dve.tensor_tensor(prod[:, h * GE:(h + 1) * GE, :],
                                            r[:, :, h * GE:(h + 1) * GE].rearrange("p k e -> p e k"),
                                            wq[:, h:h + 1, :].broadcast_to([QT, GE, KS]), ALU.mult)
                ins.then_inc(rows_used, 1)
                dve.wait_ge(own, own_t.value())
                step(own_t, dve.tensor_scalar(den[:], den[:], 1.0e-16, None, ALU.add))
                dve.wait_ge(rows_used, c * TPC + (q + 1))
                own_t.inc(dve.reciprocal(den[:], den[:]))
                step(own_t, dve.tensor_reduce(agg[:, q], prod[:], AX.X, ALU.add))
                step(own_t, dve.tensor_tensor(agg[:, q].rearrange("p (h e) -> p h e", h=GH),
                                              agg[:, q].rearrange("p (h e) -> p h e", h=GH),
                                              den[:].unsqueeze(2).broadcast_to([QT, GH, GE]), ALU.mult))

            def gates(own_t, c):
                def wide(t):
                    return t.unsqueeze(2).broadcast_to([QT, TPC, GF])

                def every(i):
                    return bg[:, i:i + 1].broadcast_to([QT, TPC, GF])
                step(own_t, dve.tensor_tensor(agg[:], agg[:], every(0), ALU.add))
                step(own_t, dve.tensor_reduce(mean[:], agg[:], AX.X, ALU.add))
                step(own_t, dve.tensor_scalar(mean[:], mean[:], 1.0 / GF, None, ALU.mult))
                step(own_t, dve.tensor_tensor(agg[:], agg[:], wide(mean[:]), ALU.subtract))
                step(own_t, dve.tensor_tensor(g16[:], agg[:], agg[:], ALU.mult))
                dve.tensor_reduce(var[:], g16[:], AX.X, ALU.add).then_inc(var_ok, 1)
                dve.wait_ge(root_ok, c + 1)
                step(own_t, dve.reciprocal(var[:], var[:]))
                step(own_t, dve.tensor_tensor(agg[:], agg[:], wide(var[:]), ALU.mult))
                step(own_t, dve.tensor_tensor(agg[:], agg[:], every(1), ALU.mult))
                step(own_t, dve.tensor_tensor(agg[:], agg[:], every(2), ALU.add))
                step(own_t, dve.tensor_reduce(sc[:], agg[:].rearrange("p t (h e) -> p t e h", h=GH), AX.X, ALU.add))
                step(own_t, dve.tensor_scalar(sc[:], sc[:], 1.0 / GH, None, ALU.mult))
                first = True
                for e in range(GE):
                    rest = [o for o in range(GE) if o != e]
                    for o in rest:
                        op = ALU.is_ge if o < e else ALU.is_gt
                        if o == rest[0]:
                            step(own_t, dve.tensor_tensor(beat[:, :, e:e + 1], sc[:, :, o:o + 1], sc[:, :, e:e + 1], op))
                        else:
                            step(own_t, dve.tensor_tensor(cmp[:], sc[:, :, o:o + 1], sc[:, :, e:e + 1], op))
                            step(own_t, dve.tensor_tensor(beat[:, :, e:e + 1], beat[:, :, e:e + 1], cmp[:], ALU.add))
                step(own_t, dve.tensor_scalar(beat[:], beat[:], 2.0, None, ALU.is_lt))
                step(own_t, dve.tensor_reduce(mean[:], sc[:], AX.X, ALU.max))
                dve.tensor_tensor(sc[:], sc[:], mean[:].unsqueeze(2).broadcast_to([QT, TPC, GE]), ALU.subtract)\
                    .then_inc(sc_ok, 1)
                dve.wait_ge(gexp_ok, c + 1)
                step(own_t, dve.tensor_tensor(gate[:], gate[:], beat[:], ALU.mult))
                step(own_t, dve.tensor_reduce(gsum[:], gate[:], AX.X, ALU.add))
                step(own_t, dve.reciprocal(gsum[:], gsum[:]))
                step(own_t, dve.tensor_tensor(gate[:], gate[:], gsum[:].unsqueeze(2).broadcast_to([QT, TPC, GE]),
                                              ALU.mult))

            def chunk(own_t, c, with_experts):
                for q in range(TPC):
                    if with_experts:
                        experts(own_t, c - 1, q)
                    node_tile(own_t, c, q, c * (TPC // 2) + q // 2, q % 2)
                gates(own_t, c)

            t = Tally(own, 0)
            chunk(t, 0, False)
            base = t.k
            steps = base + 2 * 0 + GE + 1
            with dve.Fori(1, NCH * B) as c:
                t = Tally(own, (c - 1) * steps + base)
                chunk(t, c, True)
                assert t.k == steps, (t.k, steps)
            t = Tally(own, (NCH * B - 1) * steps + base)
            for e in range(GE):
                experts(t, NCH * B - 1, e)


def key_weights():
    along = np.bincount(np.pad(np.arange(SIDE), 3, mode="reflect"), minlength=SIDE)
    w = np.zeros(KPAD, np.float32)
    w[:NTOK] = np.outer(along, along).reshape(-1)
    return np.ascontiguousarray(w.reshape(KT, P).T)


_INS = {"x": "x", "Wq": "L0_conv_Wq", "bq": "L0_conv_bq", "Wk": "L0_conv_Wk", "bk": "L0_conv_bk", "Wv": "L0_conv_Wv",
        "bv": "L0_conv_bv", "gamma": "L0_conv_gamma", "Wq1": "L1_attn_Wq", "bq1": "L1_attn_bq", "Wk1": "L1_attn_Wk",
        "bk1": "L1_attn_bk", "Wv1": "L1_attn_Wv", "bv1": "L1_attn_bv", "Wgat": "L1_ffn_W_gat",
        "att_src": "L1_ffn_att_src", "att_dst": "L1_ffn_att_dst", "b_gat": "L1_ffn_b_gat",
        "ln_gamma": "L1_ffn_ln_gamma", "ln_beta": "L1_ffn_ln_beta", "W1": "L1_ffn_W1", "b1": "L1_ffn_b1",
        "W2": "L1_ffn_W2", "b2": "L1_ffn_b2", "edge": "L1_ffn_edge_index"}


def kernel(**inputs):
    from concourse import bacc
    from concourse.bass_utils import run_bass_kernel_spmd

    nc = bacc.Bacc("TRN2", target_bir_lowering=False, num_devices=1)
    arrays = {f"in_{n}": np.ascontiguousarray(inputs[full]) for n, full in _INS.items()}
    arrays["in_mult"] = key_weights()
    a = {n[3:]: nc.dram_tensor(n, v.shape, mybir.dt.from_np(v.dtype), kind="ExternalInput").ap()
         for n, v in arrays.items()}
    out = nc.dram_tensor("out_x", (B, SIDE, SIDE, C), F32, kind="ExternalOutput").ap()
    build(nc, a, out)
    r = run_bass_kernel_spmd(nc, [arrays], core_ids=[0])
    return r.results[0]["out_x"]
```

```python
import numpy as np

import concourse.bass as bass
from concourse import mybir
from contextlib import ExitStack

F32 = mybir.dt.float32
BF16 = mybir.dt.bfloat16
I32 = mybir.dt.int32
U32 = mybir.dt.uint32
ALU = mybir.AluOpType
ACT = mybir.ActivationFunctionType
AX = mybir.AxisListType

P = 128
B, SIDE, C = 2, 56, 256
NTOK = SIDE * SIDE
M = B * NTOK
HEADS, HD = 8, 32
CH = 448
NCH = NTOK // CH
QT = 112
TPC = CH // QT
TILES = M // QT
KT = (NTOK + P - 1) // P
KPAD = KT * P
VW = HD + 1
NIT = B * HEADS * NCH
EDGES = 1048576
ECOLS = EDGES // P
GC = 7
EPI = 11
ROWS_AT, COUNT_AT = 2, 4
SLOTS = EPI + COUNT_AT
ITC = EPI * GC
ALLC = NIT * ITC
PG = 56
PC = PG * GC
NPIECE = ALLC // PC
FULLP = ECOLS // PC
K = 36
DHI = M // P
BIG = 1.0e7
GH, GE = 4, 4
GF = GH * GE
ROW = GF + 2 * GH
SW = 2 * GH + GF
GENG = 8
GLEN = ALLC // GENG
LOW = -1.0e30
FF = 512
LN_EPS = 1e-5


class Step:

    def __init__(self, n, par, half, pair, b, h, slot, c, next_slot, next_c):
        self.n, self.par, self.half, self.pair = n, par, half, pair
        self.b, self.h, self.slot, self.c = b, h, slot, c
        self.next_slot, self.next_c = next_slot, next_c


class Tally:

    def __init__(self, sem, base=0):
        self.sem, self.base, self.k = sem, base, 0

    def inc(self, ins):
        self.k += 1
        ins.then_inc(self.sem, 1)
        return self.k

    def value(self):
        return self.base + self.k


def build(nc, a, out):
    ctx = ExitStack()
    with ctx:
        def dram(name, shape, dt):
            return nc.dram_tensor(name, shape, dt).ap()

        s = {
            "q": dram("q_parts", [3, B * C, NTOK], BF16),
            "k": dram("k_parts", [3, B * C, KPAD], BF16),
            "v": dram("v_rows", [B * HEADS, P, KT * VW], F32),
            "pay": dram("edge_payload", [P, ALLC * 4], BF16),
            "src": dram("sources_by_target", [M * K, 1], I32),
            "node": dram("node_rows", [M + 1, ROW], F32),
            "state": dram("target_states", [M + 1, SW], F32),
            "flag": dram("over_flag", [1, 1], I32),
        }
        xtok = ctx.enter_context(nc.sbuf_tensor("xtok", [QT, TILES, C], F32))
        mid = ExitStack()
        with mid:
            pos = mid.enter_context(nc.sbuf_tensor("pos", [P, ALLC + 2 * GC], BF16))
            prepare(nc, a, s, xtok, pos)
            attend(nc, a, s, xtok, pos)
        xhT = ctx.enter_context(nc.sbuf_tensor("xhT", [P, 2, M], F32))
        nodes = ctx.enter_context(nc.sbuf_tensor("nodes", [QT, TILES, ROW], F32))
        mix(nc, a, s, xtok, xhT, nodes)
        states = ctx.enter_context(nc.sbuf_tensor("states", [QT, TILES, SW], F32))
        general(nc, s, states)
        route(nc, a, s, xtok, xhT, nodes, states, out)


def prepare(nc, a, s, xtok, pos):
    ctx = ExitStack()
    with ctx:
        def sb(name, shape, dt):
            return ctx.enter_context(nc.sbuf_tensor(name, shape, dt))

        def pb(name):
            return ctx.enter_context(nc.psum_tensor(name, [P, 512], F32))

        def sem(name):
            return ctx.enter_context(nc.semaphore(name))

        xT = sb("xT", [P, 2, KPAD], F32)
        w = sb("w0", [P, 3, 2, C], F32)
        qkb = sb("qkb", [P, 2, 2], F32)
        bvb = sb("bvb", [P, C], F32)
        wk = sb("wk", [P, KT], F32)
        identf = sb("identf0", [P, P], F32)
        before = sb("before0", [P, P], BF16)
        full = sb("full", [P, 2, CH], F32)
        rest = sb("rest", [P, 2, CH], F32)
        parts = sb("parts", [P, 2, 3, CH], BF16)
        vtmp = sb("vtmp", [P, 2, C], F32)
        vrow = sb("vrow", [P, HEADS, KT, VW], F32)
        none = sb("none", [QT, TILES * K], I32)
        raw = sb("raw", [P, 2, 2, PC], I32)
        e1 = sb("e1", [P, PC], F32)
        ev = sb("ev", [P, PC], F32)
        eh = sb("eh", [P, PC], I32)
        es = sb("es", [P, PC], F32)
        esi = sb("esi", [P, PC], I32)
        esh = sb("esh", [P, PC], I32)
        pre = sb("pre", [P, PG, GC], F32)
        sums = sb("sums", [P, PG], BF16)
        pay = sb("pay0", [P, 2, PC, 4], BF16)
        p_t = [pb("p_t0"), pb("p_t1")]
        p_p = [pb("p_p0"), pb("p_p1")]
        p_v = [pb("p_v0"), pb("p_v1")]
        p_b = pb("p_base")

        x_in = [sem(f"x_in{b}") for b in range(B)]
        w_in = sem("w_in")
        const = sem("const")
        zeroed = sem("zeroed")
        turned = sem("turned")
        xt_ok = sem("xt_ok")
        proj = sem("proj")
        full_ok = sem("full_ok")
        p1_ok = sem("p1_ok")
        p2_ok = sem("p2_ok")
        rest_ok = sem("rest_ok")
        p3_ok = sem("p3_ok")
        parts_out = [sem(f"parts_out{i}") for i in range(2)]
        v_ps = sem("v_ps")
        v_sum = sem("v_sum")
        v_ok = sem("v_ok")
        v_out = sem("v_out")
        none_ok = sem("none_ok")
        none_out = sem("none_out")
        raw_in = [sem(f"raw_in{i}") for i in range(2)]
        sums_ok = sem("sums_ok")
        base_ok = sem("base_ok")
        own = sem("own0")
        pay_ok = sem("pay_ok")
        pay_out = [sem(f"pay_out{i}") for i in range(2)]

        NG = 2 * NCH
        NP = 2 * 2 * NCH
        edge_v = a["edge"].rearrange("a (p c) -> p a c", p=P)
        x_v = a["x"].rearrange("b h w c -> b (h w) c").rearrange("b (t p) c -> b p t c", p=QT)
        tb = TILES // B
        LASTC = ECOLS - FULLP * PC

        block = ctx.enter_context(nc.Block())

        @block.sync
        def _(sp):
            for b in range(B):
                sp.dma_start(xtok[:, b * tb:(b + 1) * tb, :], x_v[b]).then_inc(x_in[b], 16)
            for i, name in enumerate(("Wq", "Wk", "Wv")):
                sp.dma_start(w[:, i], a[name].rearrange("(t p) n -> p t n", p=P)).then_inc(w_in, 16)
            for i, name in enumerate(("bq", "bk")):
                sp.dma_start(qkb[:, i, :], a[name].rearrange("(m p) -> p m", p=P),
                             allow_slow_non_contiguous=True).then_inc(w_in, 16)
            sp.dma_start(bvb[:], a["bv"].partition_broadcast(P)).then_inc(w_in, 16)
            sp.dma_start(wk[:], a["mult"]).then_inc(w_in, 16)
            sp.wait_ge(none_ok, 1)
            sp.dma_start(s["src"].rearrange("(t p k) o -> p t (k o)", p=QT, k=K),
                         none[:].rearrange("p (t k) -> p t k", k=K)).then_inc(none_out, 16)
            def load_piece(i):
                n = PC if i < FULLP else LASTC
                sp.dma_start(raw[:, i % 2, :, 0:n], edge_v[:, :, i * PC:i * PC + n])\
                    .then_inc(raw_in[i % 2], 16)

            load_piece(0)
            load_piece(1)
            j = 0
            done = 0
            for b in range(B):
                for i in range(2):
                    dst = s["qk"[i]]
                    for m in range(2):
                        for c in range(NCH):
                            sp.wait_ge(p3_ok, j + 1)
                            sp.wait_ge(p2_ok, j + 1)
                            r0 = b * C + m * P
                            sp.dma_start(dst[:, r0:r0 + P, c * CH:(c + 1) * CH].rearrange("t p c -> p t c"),
                                         parts[:, j % 2]).then_inc(parts_out[j % 2], 16)
                            if i == 1 and c == 0:
                                sp.dma_start(dst[:, r0:r0 + P, NTOK:KPAD].rearrange("t p c -> p t c"),
                                             parts[:, j % 2, :, 0:KPAD - NTOK]).then_inc(parts_out[j % 2], 16)
                            j += 1
                            if (j * NPIECE) // (B * NP) > done:
                                sp.wait_ge(pay_ok, done + 1)
                                sp.dma_start(s["pay"][:, done * PC * 4:(done + 1) * PC * 4],
                                             pay[:, done % 2].rearrange("p c f -> p (c f)"))\
                                    .then_inc(pay_out[done % 2], 16)
                                if done + 2 <= FULLP:
                                    load_piece(done + 2)
                                done += 1
                sp.wait_ge(v_ok, KT * (b + 1))
                sp.dma_start(s["v"][b * HEADS:(b + 1) * HEADS].rearrange("h p n -> p h n"),
                             vrow[:].rearrange("p h t w -> p h (t w)")).then_inc(v_out, 16)
            sp.wait_ge(v_out, 16 * B)
            sp.wait_ge(none_out, 16)
            for i in range(2):
                sp.wait_ge(parts_out[i], 16 * (B * NP // 2 + (B * 2) // 2))
                sp.wait_ge(pay_out[i], 16 * (NPIECE // 2))

        @block.gpsimd
        def _(pool):
            pool.memset(identf[:], 0.0).then_inc(zeroed, 1)
            pool.memset(before[:], 1.0).then_inc(zeroed, 1)
            pool.memset(xT[:, :, NTOK:KPAD], 0.0).then_inc(const, 1)
            pool.wait_ge(zeroed, 2)
            pool.affine_select(out=identf[:], in_=identf[:], compare_op=ALU.not_equal, fill=1.0, base=0,
                               pattern=[[-1, P]], channel_multiplier=1).then_inc(const, 1)
            pool.affine_select(out=before[:], in_=before[:], compare_op=ALU.is_gt, fill=0.0, base=0,
                               pattern=[[1, P]], channel_multiplier=-1).then_inc(const, 1)
            for j in range(B * NP):
                pool.wait_ge(p1_ok, j + 1)
                if j >= 2:
                    pool.wait_ge(p2_ok, j - 1)
                pool.tensor_tensor(rest[:, j % 2], full[:, j % 2], parts[:, j % 2, 0], ALU.subtract)\
                    .then_inc(rest_ok, 1)
                pool.wait_ge(p2_ok, j + 1)
                pool.tensor_tensor(parts[:, j % 2, 2], rest[:, j % 2], parts[:, j % 2, 1], ALU.subtract)\
                    .then_inc(p3_ok, 1)

        @block.scalar
        def _(act):
            j = 0
            t = 0
            for b in range(B):
                for g in range(NG):
                    act.wait_ge(turned, t + 1)
                    if b == 1 and g == 0:
                        act.wait_ge(v_ps, KT)
                    h, c = g % 2, g // 2
                    act.activation(xT[:, h, c * CH:(c + 1) * CH], p_t[t % 2][:, 0:CH], ACT.Copy)\
                        .then_inc(xt_ok, 1)
                    t += 1
                for i in range(2):
                    for m in range(2):
                        for c in range(NCH):
                            act.wait_ge(proj, j + 1)
                            if j == 0:
                                act.wait_ge(w_in, 16 * 7)
                            if j >= 2:
                                act.wait_ge(p3_ok, j - 1)
                                act.wait_ge(rest_ok, j - 1)
                                pads = sum(1 for q in range(j - 1) if q % 2 == j % 2
                                           and (q // (2 * NCH)) % 2 == 1 and q % NCH == 0)
                                act.wait_ge(parts_out[j % 2], 16 * ((j - 2) // 2 + 1 + pads))
                            act.activation(full[:, j % 2], p_p[j % 2][:, 0:CH], ACT.Identity,
                                           bias=qkb[:, i, m:m + 1]).then_inc(full_ok, 1)
                            act.wait_ge(full_ok, j + 1)
                            act.activation(parts[:, j % 2, 0], full[:, j % 2], ACT.Copy).then_inc(p1_ok, 1)
                            act.wait_ge(rest_ok, j + 1)
                            act.activation(parts[:, j % 2, 1], rest[:, j % 2], ACT.Copy).then_inc(p2_ok, 1)
                            j += 1
                for kt in range(KT):
                    n = b * KT + kt
                    act.wait_ge(v_sum, n + 1)
                    if kt == 0 and b:
                        act.wait_ge(v_out, 16 * b)
                    act.activation(vrow[:, :, kt, 0:HD], vtmp[:, n % 2].rearrange("p (h d) -> p h d", d=HD),
                                   ACT.Copy, scale=wk[:, kt:kt + 1]).then_inc(v_ok, 1)

        @block.tensor
        def _(pe):
            pe.wait_ge(const, 3)
            t = j = 0

            def base(i):
                pe.wait_ge(sums_ok, i + 1)
                pe.matmul(p_b[:, 0:PG], before[:], sums[:], start=True, stop=True).then_inc(base_ok, 1)

            done = 0
            for b in range(B):
                pe.wait_ge(x_in[b], 16)
                for g in range(NG):
                    if t >= 2:
                        pe.wait_ge(xt_ok, t - 1)
                    h, c = g % 2, g // 2
                    for q in range(TPC):
                        ins = pe.transpose(p_t[t % 2][:, q * QT:(q + 1) * QT],
                                           xtok[:, b * tb + c * TPC + q, h * P:(h + 1) * P], identf[0:QT, 0:QT])
                    ins.then_inc(turned, 1)
                    t += 1
                pe.wait_ge(w_in, 16 * 7)
                for i in range(2):
                    for m in range(2):
                        for c in range(NCH):
                            pe.wait_ge(xt_ok, b * NG + 2 * c + 2)
                            if j >= 2:
                                pe.wait_ge(full_ok, j - 1)
                            for h in range(2):
                                ins = pe.matmul(p_p[j % 2][:, 0:CH], w[:, i, h, m * P:(m + 1) * P],
                                                xT[:, h, c * CH:(c + 1) * CH], start=(h == 0), stop=(h == 1))
                            ins.then_inc(proj, 1)
                            j += 1
                            if (j * NPIECE) // (B * NP) > done:
                                base(done)
                                done += 1
                for kt in range(KT):
                    n = b * KT + kt
                    if n >= 2:
                        pe.wait_ge(v_sum, n - 1)
                    for h in range(2):
                        ins = pe.matmul(p_v[n % 2][:, 0:C], xT[:, h, kt * P:(kt + 1) * P], w[:, 2, h, :],
                                        start=(h == 0), stop=(h == 1))
                    ins.then_inc(v_ps, 1)
            assert done == NPIECE

        @block.vector
        def _(dve):
            own_t = Tally(own)
            dve.memset(none[:], M).then_inc(none_ok, 1)
            own_t.inc(dve.memset(pos[:], 0.0))
            dve.wait_ge(w_in, 16 * 7)
            vsub = [0]

            def value_sums(upto):
                while vsub[0] < min(upto, B * KT):
                    n = vsub[0]
                    if n % KT == 0:
                        if n:
                            dve.wait_ge(v_out, 16)
                        for h in range(HEADS):
                            ins = dve.tensor_copy(vrow[:, h, :, HD], wk[:])
                        own_t.inc(ins)
                    dve.wait_ge(v_ps, n + 1)
                    if n >= 2:
                        dve.wait_ge(v_ok, n - 1)
                    dve.tensor_tensor(vtmp[:, n % 2], p_v[n % 2][:, 0:C], bvb[:], ALU.add).then_inc(v_sum, 1)
                    vsub[0] += 1

            def piece(i):
                r = raw[:, i % 2]
                src, dst = r[:, 0], r[:, 1]
                py = pay[:, i % 2]
                if i < FULLP:
                    dve.wait_ge(raw_in[i % 2], 16 * (i // 2 + 1))
                else:
                    own_t.inc(dve.memset(r[:, :, LASTC if i == FULLP else 0:PC], M))
                    if i == FULLP:
                        dve.wait_ge(raw_in[i % 2], 16 * (i // 2 + 1))
                    dve.wait_ge(own, own_t.value())
                if i >= 2:
                    dve.wait_ge(pay_out[i % 2], 16 * (i // 2))
                own_t.inc(dve.tensor_scalar(e1[:], dst, 1.0, None, ALU.add))
                own_t.inc(dve.tensor_scalar(eh[:], dst, 7, None, ALU.arith_shift_right))
                own_t.inc(dve.tensor_scalar(es[:], src, 0.0, float(M), ALU.is_lt, ALU.mult))
                dve.wait_ge(own, own_t.value())
                own_t.inc(dve.tensor_scalar(ev[:], e1[:], float(M), None, ALU.is_le))
                own_t.inc(dve.tensor_copy(py[:, :, 1], eh[:]))
                own_t.inc(dve.scalar_tensor_tensor(py[:, :, 0], eh[:], -float(P), e1[:], ALU.mult, ALU.add))
                own_t.inc(dve.tensor_tensor(es[:], es[:], src, ALU.add))
                dve.wait_ge(own, own_t.value())
                own_t.inc(dve.tensor_scalar(esi[:], es[:], 0.0, float(M - 1), ALU.max, ALU.min))
                own_t.inc(dve.scalar_tensor_tensor(ev[:], e1[:], 1.0, ev[:], ALU.is_ge, ALU.mult))
                dve.wait_ge(own, own_t.value())
                own_t.inc(dve.tensor_scalar(esh[:], esi[:], 7, None, ALU.arith_shift_right))
                ev3 = ev[:].rearrange("p (g c) -> p g c", c=GC)
                own_t.inc(dve.tensor_copy(pre[:, :, 0], ev3[:, :, 0]))
                for c in range(1, GC):
                    dve.wait_ge(own, own_t.value())
                    own_t.inc(dve.tensor_tensor(pre[:, :, c], pre[:, :, c - 1], ev3[:, :, c], ALU.add))
                dve.wait_ge(own, own_t.value())
                dve.tensor_copy(sums[:], pre[:, :, GC - 1]).then_inc(sums_ok, 1)
                own_t.inc(dve.tensor_copy(py[:, :, 3], esh[:]))
                dve.scalar_tensor_tensor(py[:, :, 2], esh[:], -float(P), esi[:], ALU.mult, ALU.add)\
                    .then_inc(pay_ok, 1)
                dve.wait_ge(base_ok, i + 1)
                own_t.inc(dve.tensor_tensor(pre[:], pre[:], p_b[:, 0:PG].unsqueeze(2).broadcast_to([P, PG, GC]),
                                            ALU.add))
                dve.wait_ge(own, own_t.value())
                own_t.inc(dve.tensor_tensor(pos[:, i * PC:(i + 1) * PC], pre[:].rearrange("p g c -> p (g c)"),
                                            ev[:], ALU.mult))
                dve.wait_ge(own, own_t.value())

            for i in range(NPIECE):
                piece(i)
                if (i + 1) * 2 % NPIECE == 0:
                    value_sums(KT * (i + 1) * 2 // NPIECE)


def attend(nc, a, s, xtok, pos):
    ctx = ExitStack()
    with ctx:
        def sb(name, shape, dt):
            return ctx.enter_context(nc.sbuf_tensor(name, shape, dt))

        def pb(name):
            return ctx.enter_context(nc.psum_tensor(name, [P, 512], F32))

        def sem(name):
            return ctx.enter_context(nc.semaphore(name))

        NPROB = 5
        qa = sb("qa", [P, 2, NTOK], BF16)
        qb = sb("qb", [P, 2, NTOK], BF16)
        ka = sb("ka", [P, 2, KPAD], BF16)
        kb = sb("kb", [P, 2, KPAD], BF16)
        vv = sb("vv", [P, 2, KT, VW], F32)
        pay = sb("pay", [P, 2, ITC, 4], BF16)
        prob = sb("prob", [P, NPROB, CH], F32)
        osb = sb("osb", [P, CH], F32)
        part = sb("part", [QT, TPC, NCH], F32)
        mx = sb("mx", [QT, TPC], F32)
        fold = sb("fold", [P, VW], F32)
        identf = sb("identf", [P, P], F32)
        identb = sb("identb", [P, P], BF16)
        ones = sb("ones", [P, P], F32)
        gamma = sb("gamma", [QT, 1], F32)
        rden = sb("rden", [QT, TPC], F32)
        gden = sb("gden", [QT, TPC], F32)
        delta = sb("delta", [QT, TPC, HD], F32)
        places = sb("places", [P, P, GC], BF16)
        count1 = sb("count1", [P, P], BF16)
        countb = sb("countb", [P, DHI], BF16)
        lane1 = sb("lane1", [P, 1], F32)
        turn = sb("turn", [P, 1], F32)
        earlier = sb("earlier", [P, P], F32)
        onehot = sb("onehot", [P, 2, P, GC], BF16)
        packed = sb("packed", [P, EPI, 4], F32)
        key = sb("key", [P, EPI], F32)
        diag = sb("diag", [P, 2, P], F32)
        lo_rows = sb("lo_rows", [P, 2, P], F32)
        cols = sb("cols", [P, COUNT_AT, P + DHI], BF16)
        same = sb("same", [P, P], F32)
        found = sb("found", [P, DHI], F32)
        local = sb("local", [P, EPI], F32)
        begin = sb("begin", [P, EPI], F32)
        seen = sb("seen", [P, DHI], F32)
        rank = sb("rank", [P, EPI], F32)
        over = sb("over", [P, EPI], F32)
        empty = sb("empty", [P, EPI], F32)
        most = sb("most", [P, 4], F32)
        flag = sb("flag", [1, 1], I32)
        where = sb("where", [P, EPI], I32)
        who = sb("who", [P, EPI], I32)
        ps_a = [pb("ps_a0"), pb("ps_a1")]
        ps_s = [pb("ps_s0"), pb("ps_s1")]
        ps_o = pb("ps_o")
        ps_m = pb("ps_m")
        ps_e = pb("ps_e")
        ps_r = ctx.enter_context(nc.psum_tensor("ps_r", [P, 1024], BF16))

        zeroed = sem("zeroed1")
        const = sem("const1")
        init = sem("init1")
        head_in = [sem(f"head_in{i}") for i in range(2)]
        pay_in = [sem(f"pay_in{i}") for i in range(2)]
        lead = sem("lead")
        lead_max = sem("lead_max")
        mx_ok = sem("mx_ok")
        mrow = sem("mrow")
        first_part = sem("first_part")
        mrow_ok = sem("mrow_ok")
        score = sem("score")
        prob_ok = sem("prob_ok")
        pv = sem("pv")
        osb_ok = sem("osb_ok")
        folded = sem("folded")
        fold_read = sem("fold_read")
        own = sem("own1")
        hot_ok = sem("hot_ok")
        edge_ps = sem("edge_ps")
        edge_read = sem("edge_read")
        diag_ok = sem("diag_ok")
        cols_ok = sem("cols_ok")
        packed_ok = sem("packed_ok")
        rows_ok = sem("rows_ok")
        where_ok = sem("where_ok")
        over_ok = sem("over_ok")
        over_ps = sem("over_ps")
        flag_out = sem("flag_out")
        sent = sem("sent")
        paced = sem("paced")

        NL = TPC * NCH
        LFIRST, LSTEPS = 0, 20
        lead_at = [range(NL * (k - LFIRST) // LSTEPS, NL * (k + 1 - LFIRST) // LSTEPS)
                   if LFIRST <= k < LFIRST + LSTEPS else range(0) for k in range(KT)]
        MSTEP = 20
        slot_step = tuple(e * KT // SLOTS for e in range(SLOTS))
        assert len(slot_step) == SLOTS
        slots_at = [[e for e in range(SLOTS) if slot_step[e] == k] for k in range(KT)]
        act_at = [[e for e in range(SLOTS) if min(slot_step[e] + 2, KT - 1) == k] for k in range(KT)]
        ONE, PV0, EDGE0 = 1, NPROB, SLOTS + 1
        DMAS = 13

        def chunks(eng, body):
            with eng.Fori(0, B) as b:
                with eng.Fori(0, HEADS // 2) as hp:
                    pair = b * (HEADS // 2) + hp
                    for slot in range(2):
                        first = pair * (2 * NCH) + slot * NCH

                        def step(c2, odd):
                            c = c2 * 2 + odd
                            last = isinstance(c, int)
                            body(Step(
                                n=first + c, par=(slot * NCH + odd) % 2,
                                half=pair * NCH + (c2 + (slot * NCH + odd) // 2),
                                pair=pair, b=b, h=hp * 2 + slot, slot=slot, c=c,
                                next_slot=1 - slot if last else slot, next_c=0 if last else c + 1))
                        with eng.Fori(0, NCH // 2) as c2:
                            for odd in range(2):
                                step(c2, odd)
                        step(NCH // 2, 0)

        block = ctx.enter_context(nc.Block())

        @block.sync
        def _(sp):
            def load(h, slot):
                rows = bass.ds(h * HD, HD)

                def get(dst, src):
                    sp.dma_start(dst, src).then_inc(head_in[slot], 16)
                for g, part_ in enumerate((0, 0, 1, 1)):
                    get(qa[g * HD:(g + 1) * HD, slot, :], s["q"][part_, rows, :])
                for g, part_ in enumerate((0, 2)):
                    get(qb[g * HD:(g + 1) * HD, slot, :], s["q"][part_, rows, :])
                for g, part_ in enumerate((0, 1, 0, 1)):
                    get(ka[g * HD:(g + 1) * HD, slot, :], s["k"][part_, rows, :])
                for g, part_ in enumerate((2, 0)):
                    get(kb[g * HD:(g + 1) * HD, slot, :], s["k"][part_, rows, :])
                get(vv[:, slot].rearrange("p t w -> p (t w)"), s["v"][bass.ds(h, 1)].rearrange("h p n -> p (h n)"))

            def head(pair, slot, next_head):
                n0 = pair * (2 * NCH) + slot * NCH
                for c in range(NCH):
                    if c == 1:
                        sp.wait_ge(pv, n0 * KT + PV0)
                        load(next_head, 1 - slot)
                    sp.wait_ge(edge_ps, (n0 + c) * SLOTS + 1)
                    sp.dma_start(pay[:, (slot * NCH + c) % 2].rearrange("p e f -> p (e f)"),
                                 s["pay"][:, bass.ds((n0 + c) * (ITC * 4), ITC * 4)])\
                        .then_inc(pay_in[(slot * NCH + c) % 2], 16)

            load(0, 0)
            with sp.Fori(0, B * HEADS // 2 - 1) as pair:
                for slot in range(2):
                    head(pair, slot, pair * 2 + (slot + 1))
            last = B * HEADS // 2 - 1
            head(last, 0, 2 * last + 1)
            head(last, 1, 0)
            sp.wait_ge(head_in[0], 16 * DMAS * (B * HEADS // 2 + 1))
            sp.wait_ge(over_ok, 2)
            sp.dma_start(s["flag"], flag[:]).then_inc(flag_out, 16)
            sp.wait_ge(flag_out, 16)

        @block.gpsimd
        def _(pool):
            pool.dma_start(gamma[:], a["gamma"].partition_broadcast(QT)).then_inc(sent, 16)
            for t in (identf, fold):
                pool.memset(t[:], 0.0).then_inc(zeroed, 1)
            pool.memset(earlier[:], 1.0).then_inc(zeroed, 1)
            pool.wait_ge(zeroed, 3)
            pool.affine_select(out=identf[:], in_=identf[:], compare_op=ALU.not_equal, fill=1.0, base=0,
                               pattern=[[-1, P]], channel_multiplier=1).then_inc(const, 1)
            pool.affine_select(out=earlier[:], in_=earlier[:], compare_op=ALU.is_gt, fill=0.0, base=0,
                               pattern=[[-1, P]], channel_multiplier=1).then_inc(const, 1)
            pool.affine_select(out=fold[:], in_=fold[:], compare_op=ALU.not_equal, fill=1.0, base=0,
                               pattern=[[-1, VW]], channel_multiplier=1).then_inc(zeroed, 1)
            pool.wait_ge(zeroed, 4)
            pool.affine_select(out=fold[:], in_=fold[:], compare_op=ALU.not_equal, fill=1.0, base=-64,
                               pattern=[[-1, VW]], channel_multiplier=1).then_inc(const, 1)
            pool.iota(places[:], [[1, P], [0, GC]], base=1, channel_multiplier=0,
                      allow_small_or_imprecise_dtypes=True).then_inc(const, 1)
            pool.iota(count1[:], [[1, P]], base=1, channel_multiplier=0,
                      allow_small_or_imprecise_dtypes=True).then_inc(const, 1)
            pool.iota(countb[:], [[1, DHI]], base=0, channel_multiplier=0,
                      allow_small_or_imprecise_dtypes=True).then_inc(const, 1)
            pool.iota(lane1[:], [[0, 1]], base=1, channel_multiplier=1,
                      allow_small_or_imprecise_dtypes=True).then_inc(const, 1)
            past = pool.to_reg(M * K - 1)
            pool.sem_inc(paced, ONE)
            with pool.Fori(0, NIT) as n:
                pool.wait_ge(where_ok, n + 1)
                pool.wait_ge(paced, n + ONE)
                pool.tensor_tensor(turn[:], lane1[:], lane1[:], ALU.add).then_inc(paced, 1)
                for e in range(EPI):
                    pool.indirect_dma_start(s["src"], bass.IndirectOffsetOnAxis(ap=where[:, e:e + 1].bitcast(U32), axis=0),
                                            who[:, e:e + 1], None, bounds_check=past, oob_is_err=False)\
                        .then_inc(sent, 16)
            pool.wait_ge(sent, 16 * (EPI * NIT + 1))

        @block.scalar
        def _(act):
            act.wait_ge(const, 7)
            act.wait_ge(init, 8)
            act.sem_inc(prob_ok, ONE)
            act.sem_inc(rows_ok, ONE)

            def first_maxima(m, slot, c):
                act.wait_ge(mrow, m + 1)
                act.activation(qb[64:P, slot, bass.ds(c * CH, CH)], ps_m[64:P, 0:CH], ACT.Copy).then_inc(first_part, 1)

            first_maxima(0, 0, 0)

            def take_output(n):
                act.wait_ge(pv, n * KT + PV0)
                act.wait_ge(folded, n + ONE)
                act.activation(osb[:], ps_o[:, 0:CH], ACT.Copy).then_inc(osb_ok, 1)

            def body(it):
                n = it.n
                for k in range(KT):
                    act.wait_ge(score, n * KT + (k + 1))
                    act.wait_ge(pv, n * KT + (k + PV0 - NPROB + 1))
                    act.activation(prob[:, k % NPROB], ps_s[(k + it.par) % 2][:, 0:CH], ACT.Exp).then_inc(prob_ok, 1)
                    if k == 1:
                        take_output(n)
                    if k == MSTEP + 2:
                        first_maxima(n + 1, it.next_slot, it.next_c)
                    for e in act_at[k]:
                        if e < EPI:
                            act.wait_ge(edge_read, n * SLOTS + (e + 1 + ONE))
                            act.activation(diag[:, e % 2], identf[:], ACT.Copy, scale=key[:, e:e + 1])\
                                .then_inc(diag_ok, 1)
                        f = e - ROWS_AT
                        if 0 <= f < EPI:
                            act.wait_ge(edge_ps, n * SLOTS + (e + 1 + EDGE0))
                            act.activation(lo_rows[:, f % 2], ps_r[:, 0:P], ACT.Copy).then_inc(rows_ok, 1)

            chunks(act, body)
            take_output(NIT)

        @block.tensor
        def _(pe):
            pe.wait_ge(const, 7)
            pe.wait_ge(init, 8)

            pe.sem_inc(pv, PV0)
            pe.sem_inc(folded, ONE)
            pe.sem_inc(edge_ps, EDGE0)

            def leading(m, slot, c, js, first=False):
                for j in js:
                    q, kc = j // NCH, j % NCH
                    if not (first and j < 2):
                        pe.wait_ge(lead_max, m * NL + (j - 1 if j >= 2 else 0))
                    pe.matmul(ps_a[j % 2][0:QT, 0:CH], qa[:, slot, bass.ds(c * CH + q * QT, QT)],
                              ka[:, slot, kc * CH:(kc + 1) * CH], start=True, stop=True).then_inc(lead, 1)

            def max_rows(m):
                pe.wait_ge(mx_ok, m + 1)
                for q in range(TPC):
                    ins = pe.matmul(ps_m[:, q * QT:(q + 1) * QT], mx[:, q:q + 1].broadcast_to([QT, P]),
                                    identf[0:QT, 0:QT], start=True, stop=True)
                ins.then_inc(mrow, 1)

            def fold_heads(n):
                pe.wait_ge(osb_ok, n + 1)
                for q in range(TPC):
                    ins = pe.matmul(ps_m[0:QT, q * VW:(q + 1) * VW], osb[:, q * QT:(q + 1) * QT], fold[:],
                                    start=True, stop=True)
                ins.then_inc(folded, 1)

            def scores(n, par, slot, c, k):
                pe.wait_ge(prob_ok, n * KT + (k - 1 + ONE))
                ps = ps_s[(k + par) % 2][:, 0:CH]
                qs = bass.ds(c * CH, CH)
                pe.matmul(ps, ka[:, slot, k * P:(k + 1) * P], qa[:, slot, qs], start=True, stop=False)
                pe.matmul(ps, kb[:, slot, k * P:(k + 1) * P], qb[:, slot, qs], start=False, stop=True)\
                    .then_inc(score, 1)

            def edge_slot(it, e):
                n = it.n
                pe.wait_ge(edge_read, n * SLOTS + (e + ONE))
                if e < EPI:
                    if e == 0:
                        pe.wait_ge(pay_in[it.par], it.half * 16 + 16)
                    pe.wait_ge(hot_ok, n * EPI + (e + 1))
                    for g in range(GC):
                        ins = pe.matmul(ps_e[:, 0:4], onehot[:, e % 2, :, g],
                                        pay[:, it.par, e * GC + g, :],
                                        start=(g == 0), stop=(g == GC - 1))
                f = e - ROWS_AT
                if 0 <= f < EPI:
                    pe.wait_ge(diag_ok, n * EPI + (f + 1))
                    ins = pe.matmul(ps_e[:, 8:8 + P], ones[:], diag[:, f % 2], start=True, stop=True)
                    pe.wait_ge(cols_ok, n * EPI + (f + 1))
                    pe.wait_ge(rows_ok, n * EPI + (f + ONE))
                    ins = pe.transpose(ps_r[:, 0:P], cols[:, f % COUNT_AT, 0:P], identb[:])
                f = e - COUNT_AT
                if f >= 0:
                    pe.wait_ge(rows_ok, n * EPI + (f + 1 + ONE))
                    pe.matmul(ps_e[:, 144:144 + DHI], lo_rows[:, f % 2], seen[:], start=True, stop=True)
                    ins = pe.matmul(ps_e[:, 200:200 + DHI], cols[:, f % COUNT_AT, 0:P], cols[:, f % COUNT_AT, P:P + DHI],
                                    start=True, stop=True)
                ins.then_inc(edge_ps, 1)

            def attend_values(n, slot, k):
                pe.wait_ge(prob_ok, n * KT + (k + 1 + ONE))
                o = 64 * (k % 2)
                pe.matmul(ps_o[o:o + VW, 0:CH], vv[:, slot, k], prob[:, k % NPROB], start=(k < 2), stop=(k >= KT - 2),
                          skip_group_check=True).then_inc(pv, 1)

            pe.wait_ge(head_in[0], 16 * DMAS)
            leading(0, 0, 0, range(NL), first=True)
            max_rows(0)
            pe.wait_ge(mrow_ok, 1)
            pe.wait_ge(prob_ok, ONE)
            for k in range(2):
                qs = slice(0, CH)
                pe.matmul(ps_s[k][:, 0:CH], ka[:, 0, k * P:(k + 1) * P], qa[:, 0, qs], start=True, stop=False)
                pe.matmul(ps_s[k][:, 0:CH], kb[:, 0, k * P:(k + 1) * P], qb[:, 0, qs], start=False, stop=True)\
                    .then_inc(score, 1)

            def body(it):
                n = it.n
                for k in range(KT):
                    if k == 1 and it.next_slot != it.slot:
                        pe.wait_ge(head_in[it.next_slot], (it.pair + (1 + it.slot)) * (16 * DMAS))
                    if k + 2 < KT:
                        scores(n, it.par, it.slot, it.c, k + 2)
                    else:
                        if k + 2 == KT:
                            pe.wait_ge(mrow_ok, n + 2)
                        scores(n + 1, 1 - it.par, it.next_slot, it.next_c, k + 2 - KT)
                    for e in slots_at[k]:
                        edge_slot(it, e)
                    leading(n + 1, it.next_slot, it.next_c, lead_at[k][:1])
                    if k == 0:
                        fold_heads(n)
                    attend_values(n, it.slot, k)
                    leading(n + 1, it.next_slot, it.next_c, lead_at[k][1:])
                    if k == MSTEP:
                        pe.wait_ge(fold_read, n + ONE)
                        max_rows(n + 1)

            chunks(pe, body)
            fold_heads(NIT)
            pe.wait_ge(over_ok, 1)
            pe.matmul(ps_e[0:1, 0:1], most[:, 0:1], ones[:, 0:1], start=True, stop=True).then_inc(over_ps, 1)

        @block.vector
        def _(dve):
            dve.memset(ones[:], 1.0).then_inc(init, 1)
            dve.memset(seen[:], 0.0).then_inc(init, 1)
            dve.memset(ps_o[:], 0.0).then_inc(init, 1)
            dve.memset(kb[64:P, :, :], 0.0).then_inc(init, 1)
            dve.memset(qb[64:P, :, :], 0.0).then_inc(init, 1)
            dve.wait_ge(init, 5)
            dve.memset(kb[64:65, :, :], -1.0).then_inc(init, 1)
            dve.memset(kb[96:97, :, :], -1.0).then_inc(init, 1)
            dve.wait_ge(const, 7)
            dve.tensor_copy(identb[:], identf[:]).then_inc(init, 1)
            dve.wait_ge(init, 8)
            dve.sem_inc(edge_read, ONE)
            dve.sem_inc(fold_read, ONE)

            def places_of(col, e):
                dve.tensor_tensor(onehot[:, e % 2], pos[:, col].unsqueeze(1).broadcast_to([P, P, GC]), places[:],
                                  ALU.is_equal).then_inc(hot_ok, 1)

            def maxima(m, js):
                for j in js:
                    q, kc = j // NCH, j % NCH
                    dve.wait_ge(lead, m * NL + (j + 1))
                    dve.tensor_reduce(part[:, q, kc:kc + 1], ps_a[j % 2][0:QT, 0:CH], AX.X, ALU.max)\
                        .then_inc(lead_max, 1)

            def max_of_parts(m):
                dve.wait_ge(lead_max, (m + 1) * NL)
                if not isinstance(m, int):
                    dve.wait_ge(mrow, m)
                dve.tensor_reduce(mx[:], part[:], AX.X, ALU.max).then_inc(mx_ok, 1)

            def max_parts(own_t, m, slot, c):
                cs = bass.ds(c * CH, CH)
                dve.wait_ge(mrow, m + 1)
                dve.wait_ge(first_part, m + 1)
                dve.tensor_tensor(qb[96:P, slot, cs], ps_m[96:P, 0:CH], qb[96:P, slot, cs], ALU.subtract)\
                    .then_inc(mrow_ok, 1)

            def edge_read_slot(n, e):
                dve.wait_ge(edge_ps, n * SLOTS + (e + 1 + EDGE0))
                dve.wait_ge(edge_read, n * SLOTS + (e + ONE))
                if e:
                    dve.wait_ge(cols_ok, n * EPI + min(e, EPI))
                if e < EPI:
                    ins = dve.tensor_copy(packed[:, e], ps_e[:, 0:4]).then_inc(packed_ok, 1)
                f = e - ROWS_AT
                if 0 <= f < EPI:
                    ins = dve.scalar_tensor_tensor(same[:], ps_e[:, 8:8 + P], key[:, f:f + 1], earlier[:],
                                                   ALU.is_equal, ALU.mult, accum_out=local[:, f:f + 1])
                f = e - COUNT_AT
                if f >= 0:
                    dve.tensor_tensor_reduce(found[:], ps_e[:, 144:144 + DHI], cols[:, f % COUNT_AT, P:P + DHI], 1.0, 0.0,
                                             ALU.mult, ALU.add, begin[:, f:f + 1])
                    ins = dve.tensor_tensor(seen[:], seen[:], ps_e[:, 200:200 + DHI], ALU.add)
                if e < EPI:
                    dve.wait_ge(packed_ok, n * EPI + (e + 1))
                    ins = dve.scalar_tensor_tensor(key[:, e:e + 1], packed[:, e, 1:2], float(P), packed[:, e, 0:1],
                                                   ALU.mult, ALU.add)
                ins.then_inc(edge_read, 1)

            def next_places(n, e):
                if e + 2 < EPI:
                    places_of(bass.ds(n * ITC + (e + 2) * GC, GC), e + 2)
                elif EPI <= e < EPI + 2:
                    places_of(bass.ds((n + 1) * ITC + (e - EPI) * GC, GC), e - EPI)

            def place_edges(own_t, n):
                dve.wait_ge(edge_read, (n + 1) * SLOTS + ONE)
                own_t.inc(dve.tensor_tensor(rank[:], local[:], begin[:], ALU.add))
                own_t.inc(dve.tensor_scalar(empty[:], key[:], 1.0, BIG, ALU.is_lt, ALU.mult))
                dve.wait_ge(sent, n * (16 * EPI) + 16)
                dve.wait_ge(own, own_t.value())
                own_t.inc(dve.tensor_scalar(over[:], rank[:], float(K), BIG, ALU.is_ge, ALU.mult))
                own_t.inc(dve.scalar_tensor_tensor(rank[:], key[:], float(K), rank[:], ALU.mult, ALU.add))
                own_t.inc(dve.scalar_tensor_tensor(who[:], packed[:, :, 3], float(P), packed[:, :, 2], ALU.mult, ALU.add))
                dve.wait_ge(own, own_t.value())
                own_t.inc(dve.scalar_tensor_tensor(rank[:], rank[:], -float(K), empty[:], ALU.add, ALU.add))
                dve.wait_ge(own, own_t.value())
                dve.tensor_tensor(where[:], rank[:], over[:], ALU.add).then_inc(where_ok, 1)

            def add_head(own_t, n, b, h, c):
                dve.wait_ge(folded, n + (2 + ONE))
                ps = ps_m[0:QT, 0:TPC * VW].rearrange("p (t w) -> p t w", w=VW)
                own_t.inc(dve.reciprocal(rden[:], ps[:, :, HD]))
                dve.wait_ge(own, own_t.value())
                own_t.inc(dve.tensor_scalar(gden[:], rden[:], gamma[:, 0:1], None, ALU.mult))
                dve.wait_ge(own, own_t.value())
                dve.tensor_tensor(delta[:], ps[:, :, 0:HD], gden[:].unsqueeze(2).broadcast_to([QT, TPC, HD]), ALU.mult)\
                    .then_inc(fold_read, 1)
                dve.wait_ge(fold_read, n + (1 + ONE))
                dst = xtok[:, bass.ds(b * (TILES // B) + c * TPC, TPC), bass.ds(h * HD, HD)]
                own_t.inc(dve.tensor_tensor(dst, dst, delta[:], ALU.add))

            first = Tally(own)
            places_of(slice(0, GC), 0)
            places_of(slice(GC, 2 * GC), 1)
            maxima(0, range(NL))
            max_of_parts(0)
            max_parts(first, 0, 0, 0)
            dve.wait_ge(sent, 16)
            OWN = 6 + 3

            def body(it):
                n = it.n
                own_t = Tally(own, n * OWN + first.k)
                for k in range(KT):
                    for e in slots_at[k]:
                        edge_read_slot(n, e)
                    maxima(n + 1, lead_at[k][:1])
                    for e in slots_at[k]:
                        next_places(n, e)
                    maxima(n + 1, lead_at[k][1:])
                    for e in slots_at[k]:
                        if e < EPI:
                            dve.wait_ge(edge_read, n * SLOTS + (e + 1 + ONE))
                            dve.tensor_scalar(cols[:, e % COUNT_AT, 0:P], count1[:], packed[:, e, 0:1], None, ALU.is_equal)
                            dve.tensor_scalar(cols[:, e % COUNT_AT, P:P + DHI], countb[:], packed[:, e, 1:2], None, ALU.is_equal)\
                                .then_inc(cols_ok, 1)
                    if k == LFIRST + LSTEPS - 1:
                        max_of_parts(n + 1)
                    if k == MSTEP:
                        max_parts(own_t, n + 1, it.next_slot, it.next_c)
                place_edges(own_t, n)
                add_head(own_t, n, it.b, it.h, it.c)
                assert own_t.k == OWN, own_t.k

            chunks(dve, body)
            base = Tally(own, NIT * OWN + first.k)
            dve.wait_ge(own, base.value())
            dve.wait_ge(edge_read, NIT * SLOTS + ONE)
            base.inc(dve.tensor_reduce(most[:, 0:1], pos[:], AX.X, ALU.max))
            base.inc(dve.tensor_reduce(most[:, 1:2], seen[:], AX.X, ALU.max))
            dve.wait_ge(own, base.value())
            base.inc(dve.tensor_scalar(most[:, 2:3], most[:, 0:1], float(P), None, ALU.is_gt))
            base.inc(dve.tensor_scalar(most[:, 3:4], most[:, 1:2], float(K), None, ALU.is_gt))
            dve.wait_ge(own, base.value())
            dve.tensor_tensor(most[:, 0:1], most[:, 2:3], most[:, 3:4], ALU.add).then_inc(over_ok, 1)
            dve.wait_ge(over_ps, 1)
            dve.tensor_copy(flag[:], ps_e[0:1, 0:1]).then_inc(over_ok, 1)


def mix(nc, a, s, xtok, xhT, nodes):
    ctx = ExitStack()
    with ctx:
        def sb(name, shape, dt=F32):
            return ctx.enter_context(nc.sbuf_tensor(name, shape, dt))

        def pb(name):
            return ctx.enter_context(nc.psum_tensor(name, [P, 512], F32))

        def sem(name):
            return ctx.enter_context(nc.semaphore(name))

        w = sb("w1", [P, 3, 2, C])
        wT = sb("wT", [P, 2, 3, C])
        wb = sb("w1b", [QT, 3, C])
        wg = sb("wg", [P, 2, GF])
        att = sb("att", [QT, 2, GF])
        ident = sb("ident1", [P, P])
        stats = sb("stats", [QT, 4, nc.vector.BN_STATS_DIM])
        mv = sb("mv", [QT, TILES, 2])
        eps = sb("eps", [QT, 1])
        rstd = sb("rstd", [QT, TILES])
        shift = sb("shift", [QT, TILES])
        xn = sb("xn", [QT, 2, 2, C])
        xnT = sb("xnT", [P, 2, 4, QT])
        qk = sb("qk", [QT, 2, 2, 2, C])
        v = sb("v", [QT, 2, 2, C])
        dots = sb("dots", [QT, C])
        score = sb("score", [QT, 2, 2])
        top = sb("top", [QT, 2])
        wexp = sb("wexp", [QT, 2, 2])
        wsum = sb("wsum", [QT, 2])
        prod = sb("prod1", [QT, TILES, GF])
        last = sb("last", [1, ROW])
        ps_t = [pb("ps_t0"), pb("ps_t1")]
        ps_qk = [pb("ps_qk0"), pb("ps_qk1")]
        ps_v = [pb("ps_v0"), pb("ps_v1")]

        w_in = sem("w1_in")
        const = sem("const2")
        wturn = sem("wturn")
        wT_ok = sem("wT_ok")
        own = sem("own2")
        mv_ok = sem("mv_ok")
        var_ok = sem("var_ok")
        root_ok = sem("root_ok")
        norm_ok = sem("norm_ok")
        xn_ok = sem("xn_ok")
        turned = sem("turned1")
        xnT_ok = sem("xnT_ok")
        qk_ps = sem("qk_ps")
        v_ps = sem("v1_ps")
        qk_ok = sem("qk_ok")
        v_ok = sem("v1_ok")
        shifted = sem("shifted")
        exp_ok = sem("exp1_ok")
        mixed = sem("mixed")
        feat = sem("feat")
        feat_ok = sem("feat_ok")
        node_ok = sem("node_ok")
        node_out = sem("node_out")
        HT = TILES // B
        ONE = 1
        block = ctx.enter_context(nc.Block())

        @block.sync
        def _(sp):
            for i, n in enumerate(("Wq1", "Wk1", "Wv1")):
                sp.dma_start(w[:, i], a[n].rearrange("(t p) f -> p t f", p=P)).then_inc(w_in, 16)
            for i, n in enumerate(("bq1", "bk1", "bv1")):
                sp.dma_start(wb[:, i], a[n].partition_broadcast(QT)).then_inc(w_in, 16)
            sp.dma_start(wg[:], a["Wgat"].rearrange("(t p) f -> p t f", p=P)).then_inc(w_in, 16)
            for i, n in enumerate(("att_src", "att_dst")):
                sp.dma_start(att[:, i], a[n].rearrange("h e -> (h e)").partition_broadcast(QT)).then_inc(w_in, 16)
            sp.wait_ge(node_ok, 2)
            sp.dma_start(s["node"][0:M].rearrange("(t p) r -> p t r", p=QT), nodes[:]).then_inc(node_out, 16)
            sp.dma_start(s["node"][M:M + 1], last[:]).then_inc(node_out, 16)
            sp.wait_ge(node_out, 32)

        @block.gpsimd
        def _(pool):
            pool.memset(ident[:], 0.0).then_inc(const, 1)
            pool.memset(last[:, 0:GF], 0.0).then_inc(const, 1)
            pool.memset(last[:, GF:GF + GH], -1.0e30).then_inc(const, 1)
            pool.memset(last[:, GF + GH:ROW], 0.0).then_inc(const, 1)
            pool.memset(eps[:], LN_EPS).then_inc(const, 1)
            pool.wait_ge(const, 5)
            pool.affine_select(out=ident[:], in_=ident[:], compare_op=ALU.not_equal, fill=1.0, base=0,
                               pattern=[[-1, P]], channel_multiplier=1).then_inc(const, 1)

            def normed(dst, t):
                return pool.tensor_scalar(dst, xtok[:, t, :], rstd[:, t:t + 1], shift[:, t:t + 1], ALU.mult, ALU.add)

            pool.wait_ge(norm_ok, 1)
            for t in range(HT):
                if t >= 2:
                    pool.wait_ge(turned, t - 1)
                for img in range(2):
                    ins = normed(xn[:, t % 2, img], t + img * HT)
                ins.then_inc(xn_ok, 1)
            pool.wait_ge(norm_ok, 2)
            for t in range(TILES):
                pool.wait_ge(turned, HT + t - 1)
                normed(xn[:, t % 2, 0], t).then_inc(xn_ok, 1)

        @block.scalar
        def _(act):
            for i in range(3):
                act.wait_ge(wturn, i + 1)
                act.activation(wT[:, :, i, :],
                               ps_t[i % 2][:, 0:512].rearrange("p (h n) -> p h n", h=2), ACT.Copy)\
                    .then_inc(wT_ok, 1)
            act.sem_inc(xnT_ok, ONE)
            act.wait_ge(const, 6)
            act.wait_ge(var_ok, 1)
            act.activation(rstd[:], mv[:, :, 1], ACT.Sqrt, bias=eps[:, 0:1]).then_inc(root_ok, 1)
            with act.Fori(0, HT // 2) as i:
                for par in range(2):
                    n = i * 2 + par
                    act.wait_ge(turned, n + 1)
                    act.wait_ge(v_ps, i * 2 + ONE)
                    act.activation(xnT[:, par].rearrange("p b q -> p (b q)"), ps_t[par][:, 0:4 * QT], ACT.Copy)\
                        .then_inc(xnT_ok, 1)
                    act.wait_ge(shifted, n + 1)
                    act.activation(wexp[:], score[:], ACT.Exp).then_inc(exp_ok, 1)
            act.wait_ge(var_ok, 2)
            act.activation(rstd[:], mv[:, :, 1], ACT.Sqrt, bias=eps[:, 0:1]).then_inc(root_ok, 1)
            with act.Fori(0, HT) as i:
                for par in range(2):
                    n = i * 2 + par
                    act.wait_ge(turned, n + (HT + 1))
                    act.wait_ge(feat, i * 2 + ONE)
                    src = ps_t[par][:, 0:2 * QT].rearrange("p (h q) -> p h q", h=2)
                    act.activation(xnT[:, par, 0:2], src, ACT.Copy).then_inc(xnT_ok, 1)
                    act.activation(xhT[:, :, bass.ds(n * QT, QT)], src, ACT.Copy).then_inc(xnT_ok, 1)

        @block.tensor
        def _(pe):
            pe.wait_ge(const, 6)
            pe.wait_ge(w_in, 16 * 9)
            for i in range(3):
                if i == 2:
                    pe.wait_ge(wT_ok, 1)
                for h in range(2):
                    for g in range(2):
                        ins = pe.transpose(ps_t[i % 2][:, h * C + g * P:h * C + (g + 1) * P],
                                           w[:, i, g, h * P:(h + 1) * P], ident[:])
                ins.then_inc(wturn, 1)
            pe.wait_ge(wT_ok, 3)
            for t in (v_ps, feat):
                pe.sem_inc(t, ONE)
            with pe.Fori(0, HT // 2) as i:
                for par in range(2):
                    n = i * 2 + par
                    pe.wait_ge(xn_ok, n + 1)
                    pe.wait_ge(xnT_ok, i * 2 + (par - 1 if par else 0) + ONE)
                    for img in range(2):
                        for h in range(2):
                            j = img * 2 + h
                            ins = pe.transpose(ps_t[par][:, j * QT:(j + 1) * QT], xn[:, par, img, h * P:(h + 1) * P],
                                               ident[0:QT, 0:QT])
                    ins.then_inc(turned, 1)
                    pe.wait_ge(xnT_ok, n + 1 + ONE)
                    for img in range(2):
                        pe.wait_ge(qk_ok, n * 2 + ONE)
                        for h in range(2):
                            ins = pe.matmul(ps_qk[img][0:QT, 0:2 * C], xnT[:, par, img * 2 + h],
                                            wT[:, h, 0:2].rearrange("p i n -> p (i n)"), start=(h == 0), stop=(h == 1))
                        ins.then_inc(qk_ps, 1)
                    pe.wait_ge(v_ok, i * 2 + ONE)
                    for img in range(2):
                        for h in range(2):
                            ins = pe.matmul(ps_v[par][0:QT, img * C:(img + 1) * C], xnT[:, par, img * 2 + h],
                                            wT[:, h, 2], start=(h == 0), stop=(h == 1))
                    ins.then_inc(v_ps, 1)
            with pe.Fori(0, HT) as i:
                for par in range(2):
                    n = i * 2 + par
                    pe.wait_ge(xn_ok, n + (HT + 1))
                    pe.wait_ge(xnT_ok, i * 4 + HT + ONE)
                    for h in range(2):
                        ins = pe.transpose(ps_t[par][:, h * QT:(h + 1) * QT], xn[:, par, 0, h * P:(h + 1) * P],
                                           ident[0:QT, 0:QT])
                    ins.then_inc(turned, 1)
                    pe.wait_ge(xnT_ok, n * 2 + (HT + 1) + ONE)
                    pe.wait_ge(feat_ok, i * 2 + ONE)
                    for h in range(2):
                        ins = pe.matmul(ps_qk[par][0:QT, 0:GF], xnT[:, par, h], wg[:, h], start=(h == 0), stop=(h == 1))
                    ins.then_inc(feat, 1)

        @block.vector
        def _(dve):
            def moments(base, k):
                for t in range(0, TILES, 4):
                    dve.wait_ge(mv_ok, (k - 1) * TILES + t)
                    for q in range(4):
                        dve.bn_stats(stats[:, q], xtok[:, t + q, :]).then_inc(own, 1)
                    dve.wait_ge(own, base + t + 4)
                    for q in range(4):
                        dve.bn_aggr(mv[:, t + q, :], stats[:, q]).then_inc(mv_ok, 1)
                dve.wait_ge(mv_ok, k * TILES)
                dve.memset(stats[:, 0, 0:1], 0.0).then_inc(var_ok, 1)

            def scales(base, k):
                dve.wait_ge(root_ok, k)
                dve.reciprocal(rstd[:], rstd[:]).then_inc(own, 1)
                dve.wait_ge(own, base + 1)
                dve.scalar_tensor_tensor(shift[:], mv[:, :, 0], -1.0, rstd[:], ALU.mult, ALU.mult).then_inc(norm_ok, 1)

            for t in (qk_ok, v_ok, feat_ok):
                dve.sem_inc(t, ONE)
            moments(0, 1)
            scales(TILES, 1)
            base = TILES + 1
            STEPS = 2 * 2 + 3
            dve.wait_ge(w_in, 16 * 9)
            with dve.Fori(0, HT // 2) as i:
                for par in range(2):
                    n = i * 2 + par
                    t = Tally(own, n * STEPS + base)
                    for img in range(2):
                        dve.wait_ge(qk_ps, n * 2 + (img + 1))
                        dve.tensor_tensor(qk[:, par, img].rearrange("p i n -> p (i n)"), ps_qk[img][0:QT, 0:2 * C],
                                          wb[:, 0:2].rearrange("p i n -> p (i n)"), ALU.add).then_inc(qk_ok, 1)
                    dve.wait_ge(v_ps, n + 1 + ONE)
                    dve.tensor_tensor(v[:, par], ps_v[par][0:QT, 0:2 * C].rearrange("p (b n) -> p b n", b=2),
                                      wb[:, 2:3].broadcast_to([QT, 2, C]), ALU.add).then_inc(v_ok, 1)
                    dve.wait_ge(qk_ok, n * 2 + 2 + ONE)
                    for q in range(2):
                        for k in range(2):
                            dve.wait_ge(own, t.value())
                            t.inc(dve.tensor_tensor_reduce(dots[:], qk[:, par, q, 0], qk[:, par, k, 1], C ** -0.5, 0.0,
                                                           ALU.mult, ALU.add, score[:, q, k:k + 1]))
                    dve.wait_ge(own, t.value())
                    t.inc(dve.tensor_reduce(top[:], score[:], AX.X, ALU.max))
                    dve.wait_ge(own, t.value())
                    dve.tensor_tensor(score[:], score[:], top[:].unsqueeze(2).broadcast_to([QT, 2, 2]), ALU.subtract)\
                        .then_inc(shifted, 1)
                    dve.wait_ge(exp_ok, n + 1)
                    t.inc(dve.tensor_reduce(wsum[:], wexp[:], AX.X, ALU.add))
                    dve.wait_ge(own, t.value())
                    t.inc(dve.reciprocal(wsum[:], wsum[:]))
                    dve.wait_ge(own, t.value())
                    dve.tensor_tensor(wexp[:], wexp[:], wsum[:].unsqueeze(2).broadcast_to([QT, 2, 2]), ALU.mult)\
                        .then_inc(mixed, 1)
                    dve.wait_ge(mixed, n * 3 + 1)
                    dve.wait_ge(v_ok, n + 1 + ONE)
                    for k in range(2):
                        for q in range(2):
                            dst = xtok[:, bass.ds(n + q * HT, 1), :].rearrange("p t c -> p (t c)")
                            ins = dve.scalar_tensor_tensor(dst, v[:, par, k], wexp[:, q, k:k + 1], dst, ALU.mult, ALU.add)
                        ins.then_inc(mixed, 1)
                        dve.wait_ge(mixed, n * 3 + (k + 2))
            base += HT * STEPS
            moments(base, 2)
            base += TILES
            scales(base, 2)
            base += 1
            with dve.Fori(0, HT) as i:
                for par in range(2):
                    n = i * 2 + par
                    dve.wait_ge(feat, n + 1 + ONE)
                    dve.tensor_copy(nodes[:, bass.ds(n, 1), 0:GF].rearrange("p t f -> p (t f)"), ps_qk[par][0:QT, 0:GF])\
                        .then_inc(feat_ok, 1)
            dve.wait_ge(feat_ok, TILES + ONE)
            for i in range(2):
                dve.tensor_tensor(prod[:], nodes[:, :, 0:GF], att[:, i:i + 1].broadcast_to([QT, TILES, GF]), ALU.mult)\
                    .then_inc(own, 1)
                dve.wait_ge(own, base + i + 1)
                for h in range(GH):
                    ins = dve.tensor_reduce(nodes[:, :, GF + i * GH + h], prod[:, :, h * GE:(h + 1) * GE], AX.X, ALU.add)
                ins.then_inc(node_ok, 1)
                dve.wait_ge(node_ok, i + 1)


def general(nc, s, states):
    ctx = ExitStack()
    with ctx:
        def sb(name, shape, dt=F32):
            return ctx.enter_context(nc.sbuf_tensor(name, shape, dt))

        def pb(name):
            return ctx.enter_context(nc.psum_tensor(name, [P, 512], F32))

        def sem(name):
            return ctx.enter_context(nc.semaphore(name))

        payg = sb("payg", [P, ALLC, 4], BF16)
        noneg = sb("noneg", [QT, K], I32)
        neutral = sb("neutral", [QT, SW])
        flag = sb("flag_in", [1, 1], I32)
        identg = sb("identg", [P, P])
        onesg = sb("onesg", [P, P])
        turng = sb("turng", [P, 1])
        target = sb("target", [P, 1])
        inside = sb("inside", [P, 1])
        keyg = sb("keyg", [P, 1])
        source_i = sb("source_i", [P, 1], I32)
        key_i = sb("key_i", [P, 1], I32)
        row_s = sb("row_s", [P, ROW])
        row_t = sb("row_t", [P, ROW])
        old = sb("old", [P, SW])
        new = sb("new", [P, SW])
        diag = sb("diagg", [P, 1 + GH, P])
        equal = sb("equal", [P, P])
        pen = sb("pen", [P, P])
        zg = sb("zg", [P, GH])
        spread = sb("spread", [P, GH, P])
        low = sb("low", [P, 2 * GH])
        wexp = sb("wexpg", [P, 2 * GH])
        terms = sb("terms", [P, GH + GF])
        ps_k = pb("ps_k")
        ps_z = pb("ps_z")
        ps_t = pb("ps_sums")

        flag_in = sem("flag_in_ok")
        const = sem("constg")
        zeroed = sem("zeroedg")
        neutral_out = sem("neutral_out")
        none_out = sem("none_outg")
        pay_in = sem("payg_in")
        states_in = sem("states_in")
        s_in = [sem(f"s_in{g}") for g in range(GENG)]
        t_in = [sem(f"t_in{g}") for g in range(GENG)]
        old_in = [sem(f"old_in{g}") for g in range(GENG)]
        new_out = [sem(f"new_out{g}") for g in range(GENG)]
        idx_ok = sem("idx_okg")
        z_ok = sem("z_okg")
        diag_ok = sem("diag_okg")
        rows_ps = sem("rows_psg")
        low_ok = sem("low_okg")
        exp_ok = sem("exp_okg")
        terms_ok = sem("terms_okg")
        sums_ps = sem("sums_psg")
        new_ok = sem("new_okg")
        own = sem("owng")
        paced = sem("pacedg")
        block = ctx.enter_context(nc.Block())

        def columns(eng, body):
            for g in range(GENG):
                with eng.Fori(0, GLEN) as i:
                    body(g, i, i + g * GLEN)

        def if_over(eng):
            eng.wait_ge(flag_in, 16)
            return eng.If(eng.value_load(flag[0:1, 0:1], min_val=0, max_val=2 * P) > 0)

        @block.sync
        def _(sp):
            sp.dma_start(flag[:], s["flag"]).then_inc(flag_in, 16)
            sp.wait_ge(const, 5)
            sp.dma_start(s["state"][0:M].rearrange("(t p) r -> p t r", p=QT),
                         neutral[:].unsqueeze(1).broadcast_to([QT, TILES, SW])).then_inc(neutral_out, 16)
            sp.dma_start(s["state"][M:M + 1], neutral[0:1, :]).then_inc(neutral_out, 16)
            sp.wait_ge(neutral_out, 32)
            with if_over(sp):
                sp.dma_start(s["src"].rearrange("(t p k) o -> p t (k o)", p=QT, k=K),
                             noneg[:].unsqueeze(1).broadcast_to([QT, TILES, K])).then_inc(none_out, 16)
                sp.dma_start(payg[:].rearrange("p c f -> p (c f)"), s["pay"]).then_inc(pay_in, 16)
                sp.wait_ge(none_out, 16)
                sp.wait_ge(pay_in, 16)
                for g in range(GENG):
                    sp.wait_ge(new_out[g], 16 * GLEN)
            sp.dma_start(states[:], s["state"][0:M].rearrange("(t p) r -> p t r", p=QT)).then_inc(states_in, 16)
            sp.wait_ge(states_in, 16)

        @block.gpsimd
        def _(pool):
            pool.memset(noneg[:], M).then_inc(const, 1)
            pool.memset(neutral[:, 0:GH], LOW).then_inc(const, 1)
            pool.memset(neutral[:, GH:SW], 0.0).then_inc(const, 1)
            pool.memset(onesg[:], 1.0).then_inc(const, 1)
            pool.memset(identg[:], 0.0).then_inc(zeroed, 1)
            pool.wait_ge(zeroed, 1)
            pool.affine_select(out=identg[:], in_=identg[:], compare_op=ALU.not_equal, fill=1.0, base=0,
                               pattern=[[-1, P]], channel_multiplier=1).then_inc(const, 1)
            pool.wait_ge(const, 5)
            pool.sem_inc(paced, 1)

            def gather(dst, table, idx, done):
                pool.indirect_dma_start(dst, None, table, bass.IndirectOffsetOnAxis(ap=idx.bitcast(U32), axis=0))\
                    .then_inc(done, 16)

            def turn(step):
                pool.wait_ge(paced, step)
                pool.tensor_tensor(turng[:], onesg[:, 0:1], onesg[:, 0:1], ALU.add).then_inc(paced, 1)

            def body(g, i, n):
                pool.wait_ge(idx_ok, n + 1)
                turn(n * 3 + 1)
                gather(row_s[:], s["node"], source_i[:], s_in[g])
                gather(row_t[:], s["node"], key_i[:], t_in[g])
                gather(old[:], s["state"], key_i[:], old_in[g])
                pool.wait_ge(new_ok, n + 1)
                turn(n * 3 + 2)
                pool.indirect_dma_start(s["state"], bass.IndirectOffsetOnAxis(ap=key_i[:].bitcast(U32), axis=0),
                                        new[:], None).then_inc(new_out[g], 16)
                pool.wait_ge(new_out[g], i * 16 + 16)
                turn(n * 3 + 3)

            with if_over(pool):
                pool.wait_ge(neutral_out, 32)
                columns(pool, body)

        @block.scalar
        def _(act):
            act.wait_ge(const, 5)

            def body(g, i, n):
                act.wait_ge(idx_ok, n + 1)
                act.activation(diag[:, 0], identg[:], ACT.Copy, scale=keyg[:, 0:1])
                act.wait_ge(z_ok, n + 1)
                for h in range(GH):
                    ins = act.activation(diag[:, 1 + h], identg[:], ACT.Copy, scale=zg[:, h:h + 1])
                ins.then_inc(diag_ok, 1)
                act.wait_ge(low_ok, n + 1)
                act.activation(wexp[:], low[:], ACT.Exp).then_inc(exp_ok, 1)

            with if_over(act):
                columns(act, body)

        @block.tensor
        def _(pe):
            pe.wait_ge(const, 5)

            def body(g, i, n):
                pe.wait_ge(diag_ok, n + 1)
                pe.matmul(ps_k[:, 0:P], onesg[:], diag[:, 0], start=True, stop=True)
                pe.matmul(ps_z[:, 0:GH * P], onesg[:], diag[:, 1:1 + GH].rearrange("p h c -> p (h c)"),
                          start=True, stop=True).then_inc(rows_ps, 1)
                pe.wait_ge(terms_ok, n + 1)
                pe.matmul(ps_t[:, 0:GH + GF], equal[:], terms[:], start=True, stop=True).then_inc(sums_ps, 1)

            with if_over(pe):
                columns(pe, body)

        @block.vector
        def _(dve):
            def step(t, ins):
                t.inc(ins)
                dve.wait_ge(own, t.value())

            OWN = 15

            def body(g, i, n):
                t = Tally(own, n * OWN)
                col = payg[:, bass.ds(n, 1), :].rearrange("p c f -> p (c f)")
                if g == 0:
                    dve.wait_ge(pay_in, 16)
                t.inc(dve.scalar_tensor_tensor(source_i[:], col[:, 3:4], float(P), col[:, 2:3], ALU.mult, ALU.add))
                step(t, dve.scalar_tensor_tensor(target[:], col[:, 1:2], float(P), col[:, 0:1], ALU.mult, ALU.add))
                step(t, dve.tensor_scalar(inside[:], target[:], 1.0, None, ALU.is_ge))
                step(t, dve.scalar_tensor_tensor(inside[:], target[:], float(M), inside[:], ALU.is_le, ALU.mult))
                step(t, dve.scalar_tensor_tensor(keyg[:], target[:], -float(M + 1), inside[:], ALU.add, ALU.mult))
                step(t, dve.tensor_scalar(keyg[:], keyg[:], float(M), None, ALU.add))
                dve.tensor_copy(key_i[:], keyg[:]).then_inc(idx_ok, 1)
                dve.wait_ge(s_in[g], i * 16 + 16)
                dve.wait_ge(t_in[g], i * 16 + 16)
                step(t, dve.tensor_tensor(low[:, 0:GH], row_s[:, GF:GF + GH], row_t[:, GF + GH:ROW], ALU.add))
                dve.scalar_tensor_tensor(zg[:], low[:, 0:GH], 0.2, low[:, 0:GH], ALU.mult, ALU.max).then_inc(z_ok, 1)
                dve.wait_ge(rows_ps, n + 1)
                dve.wait_ge(z_ok, n + 1)
                step(t, dve.tensor_scalar(equal[:], ps_k[:, 0:P], keyg[:, 0:1], None, ALU.is_equal))
                t.inc(dve.tensor_scalar(pen[:], equal[:], -1.0, -LOW, ALU.add, ALU.mult))
                step(t, dve.tensor_tensor(spread[:], ps_z[:, 0:GH * P].rearrange("p (h c) -> p h c", h=GH),
                                          equal[:].unsqueeze(1).broadcast_to([P, GH, P]), ALU.mult))
                step(t, dve.tensor_tensor(spread[:], spread[:], pen[:].unsqueeze(1).broadcast_to([P, GH, P]), ALU.add))
                step(t, dve.tensor_reduce(new[:, 0:GH], spread[:], AX.X, ALU.max))
                dve.wait_ge(old_in[g], i * 16 + 16)
                step(t, dve.tensor_tensor(new[:, 0:GH], new[:, 0:GH], old[:, 0:GH], ALU.max))
                dve.tensor_tensor(low[:, 0:GH], zg[:], new[:, 0:GH], ALU.subtract)
                dve.tensor_tensor(low[:, GH:2 * GH], old[:, 0:GH], new[:, 0:GH], ALU.subtract).then_inc(low_ok, 1)
                dve.wait_ge(exp_ok, n + 1)
                dve.tensor_copy(terms[:, 0:GH], wexp[:, 0:GH])
                dve.tensor_tensor(terms[:, GH:GH + GF].rearrange("p (h e) -> p h e", h=GH),
                                  row_s[:, 0:GF].rearrange("p (h e) -> p h e", h=GH),
                                  wexp[:, 0:GH].unsqueeze(2).broadcast_to([P, GH, GE]), ALU.mult).then_inc(terms_ok, 1)
                t.inc(dve.tensor_tensor(new[:, GH:2 * GH], old[:, GH:2 * GH], wexp[:, GH:2 * GH], ALU.mult))
                step(t, dve.tensor_tensor(new[:, 2 * GH:SW].rearrange("p (h e) -> p h e", h=GH),
                                          old[:, 2 * GH:SW].rearrange("p (h e) -> p h e", h=GH),
                                          wexp[:, GH:2 * GH].unsqueeze(2).broadcast_to([P, GH, GE]), ALU.mult))
                dve.wait_ge(sums_ps, n + 1)
                dve.tensor_tensor(new[:, GH:SW], new[:, GH:SW], ps_t[:, 0:GH + GF], ALU.add).then_inc(new_ok, 1)
                dve.wait_ge(new_ok, n + 1)
                dve.wait_ge(new_out[g], i * 16 + 16)
                assert t.k == OWN, t.k

            with if_over(dve):
                columns(dve, body)


def route(nc, a, s, xtok, xhT, nodes, states, out):
    ctx = ExitStack()
    with ctx:
        def sb(name, shape, dt=F32):
            return ctx.enter_context(nc.sbuf_tensor(name, shape, dt))

        def pb(name, banks=1):
            return ctx.enter_context(nc.psum_tensor(name, [P, banks, 512], F32))

        def sem(name):
            return ctx.enter_context(nc.semaphore(name))

        KS = K + 1
        w1 = sb("we1", [P, GE, 2, FF])
        w2 = sb("we2", [P, GE, FF // P, C])
        b1 = sb("be1", [P, GE, FF // P])
        b2 = sb("be2", [QT, GE, C])
        bg = sb("bg", [QT, 3, GF])
        eps = sb("eps2", [QT, 1])
        turn = sb("turn2", [QT, 1])
        idx = sb("idx", [QT, 2, K], I32)
        rows = sb("rows", [QT, 2, KS, ROW])
        z = sb("z", [QT, GH, KS + 1])
        zmax = sb("zmax", [QT, GH])
        wz = sb("wz", [QT, 2, GH, KS + 1])
        den = sb("den", [QT, GH])
        sden = sb("sden", [QT, GH])
        prod = sb("prod", [QT, GF, KS + 1])
        agg = sb("agg", [QT, TPC, GF])
        g16 = sb("g16", [QT, TPC, GF])
        mean = sb("mean", [QT, TPC])
        var = sb("var", [QT, TPC])
        sc = sb("sc", [QT, TPC, GE])
        beat = sb("beat", [QT, TPC, GE])
        cmp = sb("cmp", [QT, TPC, 1])
        gate = sb("gate", [QT, TPC, GE])
        gsum = sb("gsum", [QT, TPC])
        hid = sb("hid", [P, 2, FF // P, CH])
        ps_h = [pb("ps_h0"), pb("ps_h1")]
        ps_y = [pb("ps_y0", 2), pb("ps_y1", 2)]

        w_in = sem("w2_in")
        eps_ok = sem("eps_ok")
        idx_in = [sem(f"idx_in{i}") for i in range(2)]
        rows_in = [sem(f"rows_in{i}") for i in range(2)]
        rows_used = sem("rows_used")
        own = sem("own3")
        shifted = sem("shifted2")
        exp_ok = sem("exp2_ok")
        var_ok = sem("var2_ok")
        root_ok = sem("root2_ok")
        sc_ok = sem("sc_ok")
        gexp_ok = sem("gexp_ok")
        hid_ps = sem("hid_ps")
        hid_ok = sem("hid_ok")
        y_ps = sem("y_ps")
        y_read = sem("y_read")
        chunk_ok = sem("chunk_ok")
        out_ok = sem("out_ok")
        paced = sem("paced2")
        NF = FF // P
        ONE = 1
        src_v = s["src"].rearrange("(t p k) o -> t p (k o)", p=QT, k=K)
        out_v = out.rearrange("b h w c -> (b h w) c").rearrange("(t p) c -> p t c", p=QT)
        block = ctx.enter_context(nc.Block())

        @block.sync
        def _(sp):
            sp.dma_start(w1[:], a["W1"].rearrange("e (t p) f -> p e t f", p=P)).then_inc(w_in, 16)
            sp.dma_start(w2[:], a["W2"].rearrange("e (t p) c -> p e t c", p=P)).then_inc(w_in, 16)
            sp.dma_start(b1[:], a["b1"].rearrange("e (t p) -> p e t", p=P), allow_slow_non_contiguous=True)\
                .then_inc(w_in, 16)
            sp.dma_start(b2[:], a["b2"].rearrange("e c -> (e c)").partition_broadcast(QT)
                         .rearrange("p (e c) -> p e c", e=GE)).then_inc(w_in, 16)
            for i, n in enumerate(("b_gat", "ln_gamma", "ln_beta")):
                sp.dma_start(bg[:, i], a[n].partition_broadcast(QT)).then_inc(w_in, 16)
            for par in range(2):
                sp.dma_start(idx[:, par], src_v[par]).then_inc(idx_in[par], 16)
            with sp.Fori(1, TILES // 2) as i:
                for par in range(2):
                    sp.wait_ge(rows_in[par], i * (16 * K))
                    sp.dma_start(idx[:, par], src_v[bass.ds(i * 2 + par, 1)].rearrange("t p k -> p (t k)"))\
                        .then_inc(idx_in[par], 16)
            with sp.Fori(0, NCH * B) as c:
                sp.wait_ge(chunk_ok, c + 1)
                ts = bass.ds(c * TPC, TPC)
                sp.dma_start(out_v[:, ts, :], xtok[:, ts, :]).then_inc(out_ok, 16)
            sp.wait_ge(out_ok, 16 * NCH * B)

        @block.gpsimd
        def _(pool):
            pool.memset(eps[:], LN_EPS).then_inc(eps_ok, 1)
            pool.wait_ge(eps_ok, 1)
            pool.sem_inc(paced, ONE)
            with pool.Fori(0, TILES // 2) as i:
                for par in range(2):
                    pool.wait_ge(idx_in[par], i * 16 + 16)
                    pool.wait_ge(rows_used, i * 2 + ONE)
                    pool.wait_ge(paced, i * 2 + par + ONE)
                    pool.tensor_tensor(turn[:], eps[:], eps[:], ALU.add).then_inc(paced, 1)
                    for k in range(K):
                        pool.indirect_dma_start(rows[:, par, k, :], None, s["node"],
                                                bass.IndirectOffsetOnAxis(ap=idx[:, par, k:k + 1].bitcast(U32), axis=0))\
                            .then_inc(rows_in[par], 16)

        @block.scalar
        def _(act):
            act.wait_ge(w_in, 16 * 7)
            act.wait_ge(eps_ok, 1)
            act.sem_inc(hid_ok, ONE)

            def hidden(c, e):
                for f in range(NF):
                    j = e * NF + f
                    act.wait_ge(hid_ps, c * (GE * NF) + (j + 1))
                    if f == 0:
                        act.wait_ge(y_ps, c * GE + (e - 1 if e >= 1 else 0) + ONE)
                    act.activation(hid[:, e % 2, f], ps_h[j % 2][:, 0, 0:CH], ACT.Gelu, bias=b1[:, e, f:f + 1])\
                        .then_inc(hid_ok, 1)

            def gat(c, experts):
                for q in range(TPC):
                    if experts:
                        for e in ((0, 1), (2,), (3,), ())[q]:
                            hidden(c - 1, e)
                    act.wait_ge(shifted, c * TPC + (q + 1))
                    act.activation(wz[:, q % 2], z[:], ACT.Exp).then_inc(exp_ok, 1)
                act.wait_ge(var_ok, c + 1)
                act.activation(var[:], var[:], ACT.Sqrt, scale=1.0 / GF, bias=eps[:, 0:1]).then_inc(root_ok, 1)
                act.wait_ge(sc_ok, c + 1)
                act.activation(gate[:], sc[:], ACT.Exp).then_inc(gexp_ok, 1)

            gat(0, False)
            with act.Fori(1, NCH * B) as c:
                gat(c, True)
            for e in range(GE):
                hidden(NCH * B - 1, e)

        @block.tensor
        def _(pe):
            pe.wait_ge(w_in, 16 * 7)
            pe.sem_inc(y_ps, ONE)
            with pe.Fori(0, NCH * B) as c:
                def up(e):
                    for f in range(NF):
                        j = e * NF + f
                        pe.wait_ge(hid_ok, c * (GE * NF) + (j - 1 if j >= 1 else 0) + ONE)
                        for h in range(2):
                            ins = pe.matmul(ps_h[j % 2][:, 0, 0:CH], w1[:, e, h, f * P:(f + 1) * P],
                                            xhT[:, h, bass.ds(c * CH, CH)], start=(h == 0), stop=(h == 1))
                        ins.then_inc(hid_ps, 1)

                def down(e):
                    pe.wait_ge(hid_ok, c * (GE * NF) + (e + 1) * NF + ONE)
                    pe.wait_ge(y_read, c * GE + (e - 1 if e >= 1 else 0) + ONE)
                    for q in range(TPC):
                        for f in range(NF):
                            ins = pe.matmul(ps_y[e % 2][0:QT, q // 2, (q % 2) * C:(q % 2 + 1) * C],
                                            hid[:, e % 2, f, q * QT:(q + 1) * QT], w2[:, e, f],
                                            start=(f == 0), stop=(f == NF - 1))
                    ins.then_inc(y_ps, 1)

                up(0)
                for e in range(GE):
                    if e + 1 < GE:
                        up(e + 1)
                    down(e)

        @block.vector
        def _(dve):
            dve.wait_ge(w_in, 16 * 7)
            for t in (rows_used, y_read):
                dve.sem_inc(t, ONE)

            def experts(own_t, c, e):
                ts = [xtok[:, bass.ds(c * TPC + q, 1), :].rearrange("p t c -> p (t c)") for q in range(TPC)]
                dve.wait_ge(own, own_t.value())
                for q in range(TPC):
                    ins = dve.scalar_tensor_tensor(ts[q], b2[:, e], gate[:, q, e:e + 1], ts[q], ALU.mult, ALU.add)
                own_t.inc(ins)
                dve.wait_ge(y_ps, c * GE + (e + 1) + ONE)
                dve.wait_ge(own, own_t.value())
                for q in range(TPC):
                    ins = dve.scalar_tensor_tensor(ts[q], ps_y[e % 2][0:QT, q // 2, (q % 2) * C:(q % 2 + 1) * C],
                                                   gate[:, q, e:e + 1], ts[q], ALU.mult, ALU.add)
                ins.then_inc(y_read, 1)
                dve.wait_ge(y_read, c * GE + (e + 1) + ONE)
                if e == GE - 1:
                    own_t.inc(dve.tensor_copy(gsum[:], gate[:, :, 0]))
                    dve.wait_ge(own, own_t.value())
                    dve.tensor_copy(mean[:], gate[:, :, 0]).then_inc(chunk_ok, 1)
                    dve.wait_ge(chunk_ok, c + 1)

            def step(own_t, ins):
                own_t.inc(ins)
                dve.wait_ge(own, own_t.value())

            def node_tile(own_t, c, q, i, par):
                r = rows[:, par]
                t = c * TPC + q
                mine = nodes[:, bass.ds(t, 1), :].rearrange("p t r -> p (t r)")
                own_t.inc(dve.tensor_copy(r[:, K, :], mine))
                dve.wait_ge(rows_in[par], (i + 1) * (16 * K))
                dve.wait_ge(own, own_t.value())
                st = states[:, bass.ds(t, 1), :].rearrange("p t r -> p (t r)")
                step(own_t, dve.tensor_tensor(z[:, :, 0:KS], r[:, :, GF:GF + GH].rearrange("p k h -> p h k"),
                                              mine[:, GF + GH:ROW].unsqueeze(2).broadcast_to([QT, GH, KS]), ALU.add))
                own_t.inc(dve.tensor_copy(z[:, :, KS:KS + 1], st[:, 0:GH].unsqueeze(2)))
                step(own_t, dve.scalar_tensor_tensor(z[:, :, 0:KS], z[:, :, 0:KS], 0.2, z[:, :, 0:KS], ALU.mult, ALU.max))
                step(own_t, dve.tensor_reduce(zmax[:], z[:], AX.X, ALU.max))
                dve.tensor_tensor(z[:], z[:], zmax[:].unsqueeze(2).broadcast_to([QT, GH, KS + 1]), ALU.subtract)\
                    .then_inc(shifted, 1)
                dve.wait_ge(exp_ok, c * TPC + (q + 1))
                wq = wz[:, q % 2]
                own_t.inc(dve.tensor_reduce(den[:], wq[:, :, 0:KS], AX.X, ALU.add))
                own_t.inc(dve.tensor_tensor(sden[:], wq[:, :, KS], st[:, GH:2 * GH], ALU.mult))
                own_t.inc(dve.tensor_tensor(prod[:, :, KS].rearrange("p (h e) -> p h e", h=GH),
                                            st[:, 2 * GH:SW].rearrange("p (h e) -> p h e", h=GH),
                                            wq[:, :, KS:KS + 1].broadcast_to([QT, GH, GE]), ALU.mult))
                for h in range(GH):
                    ins = dve.tensor_tensor(prod[:, h * GE:(h + 1) * GE, 0:KS],
                                            r[:, :, h * GE:(h + 1) * GE].rearrange("p k e -> p e k"),
                                            wq[:, h:h + 1, 0:KS].broadcast_to([QT, GE, KS]), ALU.mult)
                ins.then_inc(rows_used, 1)
                dve.wait_ge(own, own_t.value())
                step(own_t, dve.scalar_tensor_tensor(den[:], den[:], 1.0e-16, sden[:], ALU.add, ALU.add))
                dve.wait_ge(rows_used, c * TPC + (q + 1) + ONE)
                own_t.inc(dve.reciprocal(den[:], den[:]))
                step(own_t, dve.tensor_reduce(agg[:, q], prod[:], AX.X, ALU.add))
                step(own_t, dve.tensor_tensor(agg[:, q].rearrange("p (h e) -> p h e", h=GH),
                                              agg[:, q].rearrange("p (h e) -> p h e", h=GH),
                                              den[:].unsqueeze(2).broadcast_to([QT, GH, GE]), ALU.mult))

            def gates(own_t, c):
                def wide(t):
                    return t.unsqueeze(2).broadcast_to([QT, TPC, GF])

                def every(i):
                    return bg[:, i:i + 1].broadcast_to([QT, TPC, GF])
                step(own_t, dve.tensor_tensor(agg[:], agg[:], every(0), ALU.add))
                step(own_t, dve.tensor_reduce(mean[:], agg[:], AX.X, ALU.add))
                step(own_t, dve.tensor_scalar(mean[:], mean[:], 1.0 / GF, None, ALU.mult))
                step(own_t, dve.tensor_tensor(agg[:], agg[:], wide(mean[:]), ALU.subtract))
                step(own_t, dve.tensor_tensor(g16[:], agg[:], agg[:], ALU.mult))
                dve.tensor_reduce(var[:], g16[:], AX.X, ALU.add).then_inc(var_ok, 1)
                dve.wait_ge(root_ok, c + 1)
                step(own_t, dve.reciprocal(var[:], var[:]))
                step(own_t, dve.tensor_tensor(agg[:], agg[:], wide(var[:]), ALU.mult))
                step(own_t, dve.tensor_tensor(agg[:], agg[:], every(1), ALU.mult))
                step(own_t, dve.tensor_tensor(agg[:], agg[:], every(2), ALU.add))
                step(own_t, dve.tensor_reduce(sc[:], agg[:].rearrange("p t (h e) -> p t e h", h=GH), AX.X, ALU.add))
                step(own_t, dve.tensor_scalar(sc[:], sc[:], 1.0 / GH, None, ALU.mult))
                first = True
                for e in range(GE):
                    rest = [o for o in range(GE) if o != e]
                    for o in rest:
                        op = ALU.is_ge if o < e else ALU.is_gt
                        if o == rest[0]:
                            step(own_t, dve.tensor_tensor(beat[:, :, e:e + 1], sc[:, :, o:o + 1], sc[:, :, e:e + 1], op))
                        else:
                            step(own_t, dve.tensor_tensor(cmp[:], sc[:, :, o:o + 1], sc[:, :, e:e + 1], op))
                            step(own_t, dve.tensor_tensor(beat[:, :, e:e + 1], beat[:, :, e:e + 1], cmp[:], ALU.add))
                step(own_t, dve.tensor_scalar(beat[:], beat[:], 2.0, None, ALU.is_lt))
                step(own_t, dve.tensor_reduce(mean[:], sc[:], AX.X, ALU.max))
                dve.tensor_tensor(sc[:], sc[:], mean[:].unsqueeze(2).broadcast_to([QT, TPC, GE]), ALU.subtract)\
                    .then_inc(sc_ok, 1)
                dve.wait_ge(gexp_ok, c + 1)
                step(own_t, dve.tensor_tensor(gate[:], gate[:], beat[:], ALU.mult))
                step(own_t, dve.tensor_reduce(gsum[:], gate[:], AX.X, ALU.add))
                step(own_t, dve.reciprocal(gsum[:], gsum[:]))
                step(own_t, dve.tensor_tensor(gate[:], gate[:], gsum[:].unsqueeze(2).broadcast_to([QT, TPC, GE]),
                                              ALU.mult))

            def chunk(own_t, c, with_experts):
                for q in range(TPC):
                    if with_experts:
                        experts(own_t, c - 1, q)
                    node_tile(own_t, c, q, c * (TPC // 2) + q // 2, q % 2)
                gates(own_t, c)

            t = Tally(own, 0)
            chunk(t, 0, False)
            base = t.k
            steps = base + 2 * 0 + GE + 1
            with dve.Fori(1, NCH * B) as c:
                t = Tally(own, (c - 1) * steps + base)
                chunk(t, c, True)
                assert t.k == steps, (t.k, steps)
            t = Tally(own, (NCH * B - 1) * steps + base)
            for e in range(GE):
                experts(t, NCH * B - 1, e)


def key_weights():
    along = np.bincount(np.pad(np.arange(SIDE), 3, mode="reflect"), minlength=SIDE)
    w = np.zeros(KPAD, np.float32)
    w[:NTOK] = np.outer(along, along).reshape(-1)
    return np.ascontiguousarray(w.reshape(KT, P).T)


_INS = {"x": "x", "Wq": "L0_conv_Wq", "bq": "L0_conv_bq", "Wk": "L0_conv_Wk", "bk": "L0_conv_bk", "Wv": "L0_conv_Wv",
        "bv": "L0_conv_bv", "gamma": "L0_conv_gamma", "Wq1": "L1_attn_Wq", "bq1": "L1_attn_bq", "Wk1": "L1_attn_Wk",
        "bk1": "L1_attn_bk", "Wv1": "L1_attn_Wv", "bv1": "L1_attn_bv", "Wgat": "L1_ffn_W_gat",
        "att_src": "L1_ffn_att_src", "att_dst": "L1_ffn_att_dst", "b_gat": "L1_ffn_b_gat",
        "ln_gamma": "L1_ffn_ln_gamma", "ln_beta": "L1_ffn_ln_beta", "W1": "L1_ffn_W1", "b1": "L1_ffn_b1",
        "W2": "L1_ffn_W2", "b2": "L1_ffn_b2", "edge": "L1_ffn_edge_index"}


def kernel(**inputs):
    from concourse import bacc
    from concourse.bass_utils import run_bass_kernel_spmd

    nc = bacc.Bacc("TRN2", target_bir_lowering=False, num_devices=1)
    arrays = {f"in_{n}": np.ascontiguousarray(inputs[full]) for n, full in _INS.items()}
    arrays["in_mult"] = key_weights()
    a = {n[3:]: nc.dram_tensor(n, v.shape, mybir.dt.from_np(v.dtype), kind="ExternalInput").ap()
         for n, v in arrays.items()}
    out = nc.dram_tensor("out_x", (B, SIDE, SIDE, C), F32, kind="ExternalOutput").ap()
    build(nc, a, out)
    r = run_bass_kernel_spmd(nc, [arrays], core_ids=[0])
    return r.results[0]["out_x"]
```
